# Optimizing a Trainium2 kernel written in Bass

```python
import numpy as np
import jax
import jax.numpy as jnp

def _softmax(x, axis=-1):
    return jax.nn.softmax(x, axis=axis)

def _gelu(x):
    return jax.nn.gelu(x, approximate=True)

def _silu(x):
    return jax.nn.silu(x)

def _sigmoid(x):
    return jax.nn.sigmoid(x)

def _layernorm(x, axis=-1, eps=1e-05):
    m = jnp.mean(x, axis=axis, keepdims=True)
    v = jnp.var(x, axis=axis, keepdims=True)
    return (x - m) / jnp.sqrt(v + eps)

def _scatter_add(tgt, idx, src, axis=0):
    return tgt.at[idx].add(src)

def _segment_sum(src, seg, n):
    return jax.ops.segment_sum(src, seg, n)
kernel_name = 'mk_decoder_postln_d1_seqx_r4_4a61b1'

def setup_inputs(seed: int=0):
    np.random.seed(seed)
    _w = jnp.asarray

    def _rec_inputs():
        import jax
        import jax.numpy as jnp
        _rk = jax.random.key(seed)
        x = -7.109e-05 + 0.9999 * jax.random.normal(jax.random.fold_in(_rk, 1), (8, 112, 1024), jnp.float32)
        _lenS = 112 - jax.random.randint(jax.random.fold_in(_rk, 7), (8,), 0, max(1, 112 // 4) + 1, jnp.int32)
        _lenS2 = 375 - jax.random.randint(jax.random.fold_in(_rk, 8), (8,), 0, max(1, 375 // 4) + 1, jnp.int32)
        _ctx_4096P = jax.random.normal(jax.random.fold_in(_rk, 11), (8, 16, 1024), jnp.float32)
        _ctx_4096c = jax.random.dirichlet(jax.random.fold_in(_rk, 511), 0.3 * jnp.ones((16,), jnp.float32), (8, 375))
        _ctx_4096t = jnp.einsum('bsk,bkd->bsd', _ctx_4096c, _ctx_4096P)
        _ctx_4096t = _ctx_4096t * jax.lax.rsqrt(jnp.mean(jnp.square(_ctx_4096t)) + 1e-12) * 0.953939
        ctx_4096 = -0.00010331 + 0.999899 * (_ctx_4096t + 0.3 * jax.random.normal(jax.random.fold_in(_rk, 611), (8, 375, 1024), jnp.float32))
        return (x, ctx_4096)
    x, ctx_4096 = _rec_inputs()

    def _L0_attn_setup():
        import jax, jax.numpy as jnp
        import numpy as np
        EMBED = 1024
        HEADS = 16
        HEAD_DIM = EMBED // HEADS
        ROT = 64
        B, S = (1, 512)
        MASK_VAL = -1000000000.0

        def _rotate_every_two(x):
            r = jnp.stack((x[..., 1::2], x[..., ::2]), axis=-1)
            return r.reshape(x.shape)

        def _fixed_pos_embedding(seq_len, rot_dim):
            inv_freq = 1.0 / 10000.0 ** (jnp.arange(0, rot_dim, 2, dtype=jnp.float32) / rot_dim)
            t = jnp.arange(seq_len, dtype=jnp.float32)
            sinusoid = jnp.einsum('i,j->ij', t, inv_freq)
            return (jnp.sin(sinusoid), jnp.cos(sinusoid))

        def _apply_rotary(x, sin, cos):
            sin = jnp.repeat(sin[None, :, None, :], 2, axis=3)
            cos = jnp.repeat(cos[None, :, None, :], 2, axis=3)
            return x * cos + _rotate_every_two(x) * sin
        key = jax.random.key(seed)
        ks = jax.random.split(key, 5)
        sc = 0.02
        return {'hidden_states': jax.random.normal(ks[0], (B, S, EMBED), jnp.float32), 'Wq': jax.random.normal(ks[1], (EMBED, EMBED), jnp.float32) * sc, 'Wk': jax.random.normal(ks[2], (EMBED, EMBED), jnp.float32) * sc, 'Wv': jax.random.normal(ks[3], (EMBED, EMBED), jnp.float32) * sc, 'Wo': jax.random.normal(ks[4], (EMBED, EMBED), jnp.float32) * sc}
    _L0_attn_all = _L0_attn_setup()
    _L0_attn_in = {k: v for k, v in _L0_attn_all.items() if k in ('Wq', 'Wk', 'Wv', 'Wo')}
    del _L0_attn_all

    def _L0_xattn_setup():
        import jax, jax.numpy as jnp
        import numpy as np
        key = jax.random.key(seed)
        k1, k2 = jax.random.split(key)
        B, Lq, Lk, D = (16, 256, 512, 1024)
        query = jax.random.normal(k1, (B, Lq, D), dtype=jnp.float32)
        key_t = jax.random.normal(k2, (B, Lk, D), dtype=jnp.float32)
        return {'query': query, 'key': key_t}
    _L0_xattn_all = _L0_xattn_setup()
    _L0_xattn_in = {k: v for k, v in _L0_xattn_all.items() if k in ()}
    del _L0_xattn_all

    def _L0_ffn_setup():
        import jax, jax.numpy as jnp
        import numpy as np
        LORA_RANK = 16
        LORA_ALPHA = 16
        LORA_SCALE = LORA_ALPHA / LORA_RANK
        key = jax.random.key(seed)
        k1, k2, k3, k4, k5 = jax.random.split(key, 5)
        B, S, D_IN, D_OUT, N_LORA, R = (8, 512, 1024, 1024, 3, LORA_RANK)
        std = 1.0 / np.sqrt(D_IN)
        x = jax.random.normal(k1, (B, S, D_IN), dtype=jnp.float32)
        weight = jax.random.truncated_normal(k2, -3.0, 3.0, (D_OUT, D_IN), dtype=jnp.float32) * std
        bias = jax.random.normal(k3, (D_OUT,), dtype=jnp.float32) * 0.01
        lora_A = jax.random.normal(k4, (N_LORA, R, D_IN), dtype=jnp.float32) * std
        lora_B = jax.random.normal(k5, (N_LORA, D_OUT, R), dtype=jnp.float32) * 0.02
        lora_start_indices = jnp.arange(4, dtype=jnp.int64) * 2
        return {'x': x, 'weight': weight, 'bias': bias, 'lora_A': lora_A, 'lora_B': lora_B, 'lora_start_indices': lora_start_indices}
    _L0_ffn_all = _L0_ffn_setup()
    _L0_ffn_in = {k: v for k, v in _L0_ffn_all.items() if k in ('weight', 'bias', 'lora_A', 'lora_B', 'lora_start_indices')}
    del _L0_ffn_all
    return {'x': x, 'ctx_4096': ctx_4096, 'L0_attn_Wq': _L0_attn_in['Wq'], 'L0_attn_Wk': _L0_attn_in['Wk'], 'L0_attn_Wv': _L0_attn_in['Wv'], 'L0_attn_Wo': _L0_attn_in['Wo'], 'L0_ffn_weight': _L0_ffn_in['weight'], 'L0_ffn_bias': _L0_ffn_in['bias'], 'L0_ffn_lora_A': _L0_ffn_in['lora_A'], 'L0_ffn_lora_B': _L0_ffn_in['lora_B'], 'L0_ffn_lora_start_indices': _L0_ffn_in['lora_start_indices']}

def reference(x, ctx_4096, L0_attn_Wq, L0_attn_Wk, L0_attn_Wv, L0_attn_Wo, L0_ffn_weight, L0_ffn_bias, L0_ffn_lora_A, L0_ffn_lora_B, L0_ffn_lora_start_indices):
    import jax
    import jax.numpy as jnp

    def _L0_attn_ref(hidden_states, Wq, Wk, Wv, Wo):
        import jax, jax.numpy as jnp
        import numpy as np
        EMBED = 1024
        HEADS = 16
        HEAD_DIM = EMBED // HEADS
        ROT = 64
        B, S = (1, 512)
        MASK_VAL = -1000000000.0

        def _rotate_every_two(x):
            r = jnp.stack((x[..., 1::2], x[..., ::2]), axis=-1)
            return r.reshape(x.shape)

        def _fixed_pos_embedding(seq_len, rot_dim):
            inv_freq = 1.0 / 10000.0 ** (jnp.arange(0, rot_dim, 2, dtype=jnp.float32) / rot_dim)
            t = jnp.arange(seq_len, dtype=jnp.float32)
            sinusoid = jnp.einsum('i,j->ij', t, inv_freq)
            return (jnp.sin(sinusoid), jnp.cos(sinusoid))

        def _apply_rotary(x, sin, cos):
            sin = jnp.repeat(sin[None, :, None, :], 2, axis=3)
            cos = jnp.repeat(cos[None, :, None, :], 2, axis=3)
            return x * cos + _rotate_every_two(x) * sin
        b, s, e = hidden_states.shape
        q = (hidden_states @ Wq).reshape(b, s, HEADS, HEAD_DIM)
        k = (hidden_states @ Wk).reshape(b, s, HEADS, HEAD_DIM)
        v = (hidden_states @ Wv).reshape(b, s, HEADS, HEAD_DIM)
        sin, cos = _fixed_pos_embedding(s, ROT)
        q = jnp.concatenate([_apply_rotary(q[..., :ROT], sin, cos), q[..., ROT:]], axis=-1)
        k = jnp.concatenate([_apply_rotary(k[..., :ROT], sin, cos), k[..., ROT:]], axis=-1)
        q = q.transpose(0, 2, 1, 3)
        k = k.transpose(0, 2, 1, 3)
        v = v.transpose(0, 2, 1, 3)
        logits = jnp.einsum('bhqd,bhkd->bhqk', q, k)
        causal = jnp.tril(jnp.ones((s, s), dtype=bool))[None, None]
        logits = jnp.where(causal, logits, MASK_VAL)
        logits = logits / jnp.sqrt(jnp.float32(HEAD_DIM))
        attn = jax.nn.softmax(logits, axis=-1)
        out = jnp.einsum('bhqk,bhkd->bhqd', attn, v)
        out = out.transpose(0, 2, 1, 3).reshape(b, s, e)
        return out @ Wo

    def _L0_xattn_ref(query, key):
        import jax, jax.numpy as jnp
        import numpy as np
        a = jnp.einsum('bqd,bkd->bqk', query, key)
        e = jax.nn.softmax(a, axis=-1)
        c = jnp.einsum('bqk,bkd->bqd', e, key)
        return c

    def _L0_ffn_ref(x, weight, bias, lora_A, lora_B, lora_start_indices):
        import jax, jax.numpy as jnp
        import numpy as np
        LORA_RANK = 16
        LORA_ALPHA = 16
        LORA_SCALE = LORA_ALPHA / LORA_RANK
        y = jnp.einsum('bsd,od->bso', x, weight) + bias
        B = x.shape[0]
        seg = jnp.searchsorted(lora_start_indices, jnp.arange(B), side='right') - 1
        adapter_idx = jnp.clip(seg - 1, 0, lora_A.shape[0] - 1)
        A = lora_A[adapter_idx]
        Bw = lora_B[adapter_idx]
        lo = jnp.einsum('bsr,bor->bso', jnp.einsum('bsd,brd->bsr', x, A), Bw) * LORA_SCALE
        use_lora = (seg > 0)[:, None, None]
        return y + jnp.where(use_lora, lo, jnp.zeros((), dtype=y.dtype))
    x = _layernorm(x + _L0_attn_ref(x, L0_attn_Wq, L0_attn_Wk, L0_attn_Wv, L0_attn_Wo), axis=-1)
    x = _layernorm(x + _L0_xattn_ref(x, ctx_4096), axis=-1)
    x = _layernorm(x + _L0_ffn_ref(x, L0_ffn_weight, L0_ffn_bias, L0_ffn_lora_A, L0_ffn_lora_B, L0_ffn_lora_start_indices), axis=-1)
    return x

_drawn_inputs = setup_inputs


def setup_inputs(seed=0):
    import zlib

    import numpy as np

    out = dict(_drawn_inputs(seed))
    spreads = {}
    factors = {'L0_ffn_bias': 8.0}
    for name, (base, spread) in spreads.items():
        noise = np.random.default_rng([zlib.crc32(name.encode()), seed]).standard_normal(out[name].shape)
        drawn = base * np.exp(spread * noise) if base else spread * noise
        out[name] = jnp.asarray(drawn.astype(out[name].dtype))
    for name, factor in factors.items():
        out[name] = (out[name] * factor).astype(out[name].dtype)
    return out
```

```python
from contextlib import ExitStack

import numpy as np

import concourse.bass as bass
from concourse import mybir

F32 = mybir.dt.float32
F32R = mybir.dt.float32r
I32 = mybir.dt.int32
ALU = mybir.AluOpType
ACT = mybir.ActivationFunctionType
AX = mybir.AxisListType

P = 128
B = 8
S = 112
D = 1024
KT = D // P
HD = 64
PAIRS = D // (2 * HD)
HB = B // 2
HT = HB * S
LK = 375
LKP = LK + 1
CR = 125
CC = LK // CR
R = 16
NA = 3
RA = NA * R
BIAS_ROW = RA
EXTRA = 64
EPS = 1e-5
MASKED = -2e9
SCORE_SCALE = 1.0 / (2.0 * HD ** 0.5)


def any_yet(n):
    return not isinstance(n, int) or n > 0


def pairs_of_steps(eng, first, last):
    with eng.Fori(first, last) as m:
        yield m, 0
        yield m, 1


def build(nc, x_feat, x_tok, qkv_w, wo_w, ffn_w, ctx_feat, ctx_tok, starts, rotary, causal,
          identity, route, out):
    st = ExitStack()
    with st:
        def sb(name, shape, dt=F32, scope=st):
            return scope.enter_context(nc.sbuf_tensor(name, shape, dt))

        def sem(name):
            return st.enter_context(nc.semaphore(name))

        with ExitStack() as early:
            x_raw = sb("x_raw", [P, KT, B * S], F32, early)
        act_hi = sb("act_hi", [P, KT, B * S], F32R)
        act_lo = sb("act_lo", [P, KT, B * S], F32R)
        w_raw = [sb(f"w_raw{i}", [P, KT + 1, P]) for i in range(2)]
        w_hi = [sb(f"w_hi{i}", [P, KT + 1, P], F32R) for i in range(2)]
        w_lo = [sb(f"w_lo{i}", [P, KT + 1, P], F32R) for i in range(2)]
        y_feat = sb("y_feat", [P, 2, HT])
        ident = sb("ident", [P, P])
        mask = sb("mask", [S, S])
        turn = sb("turn", [P, S])
        stats = sb("stats", [S, B, KT, 6])
        mv = sb("mv", [S, B, 2])
        rstd = sb("rstd", [S, B, 1])
        route_c = sb("route_c", [RA, B + 1])
        starts_i = sb("starts_i", [RA, NA + 1], I32)
        starts_f = sb("starts_f", [RA, NA + 1])
        passed = sb("passed", [RA, NA + 1, B])
        sel = sb("sel", [RA, B])
        with ExitStack() as one:
            x_hi = sb("x_hi", [P, KT, B * S], F32R, one)
            x_lo = sb("x_lo", [P, KT, B * S], F32R, one)
            w_raw.append(sb("w_raw2", [P, KT, P], F32, one))
            w_hi.append(sb("w_hi2", [P, KT, P], F32R, one))
            w_lo.append(sb("w_lo2", [P, KT, P], F32R, one))
            w_mix = sb("w_mix", [P, KT, P], F32, one)
            qk = [[sb(f"{n}{i}", [P, B, S], F32, one) for n in ("q_feat", "k_feat")]
                  for i in range(2)]
            v_feat = sb("v_feat", [P, B, S], F32, one)
            v_tok = sb("v_tok", [S, B, P], F32, one)
            prob = [sb(f"prob{i}", [S, HB, S], F32, one) for i in range(4)]
            prob_t = [sb(f"prob_t{i}", [S, HB, S], F32, one) for i in range(4)]
            top = sb("top", [S, 4, HB], F32, one)
            shift = sb("shift", [S, 4, HB], F32, one)
            total = sb("total", [S, 4, HB], F32, one)
            inv = sb("inv", [S, 4, HB], F32, one)
        resid = sb("resid", [S, B, KT, P])
        with ExitStack() as three:
            cf_raw = [sb(f"cf_raw{i}", [P, KT // 2, LKP], F32, three) for i in range(2)]
            cf_hi = sb("cf_hi", [P, KT, LKP], F32R, three)
            cf_lo = sb("cf_lo", [P, KT, LKP], F32R, three)
            ct = [sb(f"ctx_tok{i}", [CR, CC, D], F32, three) for i in range(2)]
            x1 = sb("x1", [S, KT, P], F32, three)
            x2 = sb("x2", [S, KT, P], F32, three)
            x1_hi = sb("x1_hi", [P, KT, S], F32R, three)
            x1_lo = sb("x1_lo", [P, KT, S], F32R, three)
            cprob = sb("cprob", [S, LKP], F32, three)
            cprob_t = sb("cprob_t", [CR, CC, S], F32, three)
            ctop = sb("ctop", [S, 4], F32, three)
            stats2 = sb("stats2", [S, 2, 6], F32, three)
            mv2 = sb("mv2", [S, 4], F32, three)
        with ExitStack() as four:
            t_raw = sb("t_raw", [RA, B, S], F32, four)
            t_hi = sb("t_hi", [EXTRA, B, S], F32R, four)
            t_lo = sb("t_lo", [EXTRA, B, S], F32R, four)

        bank = [st.enter_context(nc.psum_tensor(f"bank{i}", [P, 512], F32)) for i in range(8)]
        PROD = bank[0:2]
        TURN = bank[2:4]
        SCORE = bank[4:6]
        HEADS = bank[6]
        SPARE = bank[7]
        X2T = [SCORE[1], SPARE]

        const_in = sem("const_in")
        x_in = [sem(f"x_in{k}") for k in range(KT)]
        x_rounded, x_rest = sem("x_rounded"), sem("x_rest")
        w_in = [sem(f"w_in{i}") for i in range(3)]
        w_mixed, w_rounded, w_rest = sem("w_mixed"), sem("w_rounded"), sem("w_rest")
        proj_done = sem("proj_done")
        qk_kept, v_kept = sem("qk_kept"), sem("v_kept")
        v_turned, v_tok_kept = sem("v_turned"), sem("v_tok_kept")
        scored, masked, topped, shifted = sem("scored"), sem("masked"), sem("topped"), sem("shifted")
        exped, inverted, normed = sem("exped"), sem("inverted"), sem("normed")
        prob_turned, prob_t_kept = sem("prob_turned"), sem("prob_t_kept")
        heads_done, heads_rounded, heads_rest = sem("heads_done"), sem("heads_rounded"), sem("heads_rest")
        lin_in = [sem(f"lin_in{i}") for i in range(2)]
        lin_rounded, lin_rest, lin_done = sem("lin_rounded"), sem("lin_rest"), sem("lin_done")
        y_kept, y_turned, y_added, y_stats = sem("y_kept"), sem("y_turned"), sem("y_added"), sem("y_stats")
        resid_in = sem("resid_in")
        norm_var, norm_std, norm_inv, norm_aggr = sem("norm_var"), sem("norm_std"), sem("norm_inv"), sem("norm_aggr")
        x1_ready, x1_kept, x1_turned = sem("x1_ready"), sem("x1_kept"), sem("x1_turned")
        x1_rounded, x1_rest = sem("x1_rounded"), sem("x1_rest")
        cf_in = [sem(f"cf_in{i}") for i in range(2)]
        ct_in = [sem(f"ct_in{i}") for i in range(2)]
        cf_rounded, cf_rest = sem("cf_rounded"), sem("cf_rest")
        cscored, ctopped, cshifted, cexped = sem("cscored"), sem("ctopped"), sem("cshifted"), sem("cexped")
        cinverted, cnormed, cturned, cprob_t_kept = sem("cinverted"), sem("cnormed"), sem("cturned"), sem("cprob_t_kept")
        cmixed, cadded, cstats, caggr = sem("cmixed"), sem("cadded"), sem("cstats"), sem("caggr")
        cvar, cstd, cinv = sem("cvar"), sem("cstd"), sem("cinv")
        x2_ready, x2_kept, x2_turned = sem("x2_ready"), sem("x2_kept"), sem("x2_turned")
        x2_rounded, x2_rest = sem("x2_rounded"), sem("x2_rest")
        routed, t_masked, t_rounded, t_rest, t_filled = sem("routed"), sem("t_masked"), sem("t_rounded"), sem("t_rest"), sem("t_filled")
        out_ready, out_stored = sem("out_ready"), sem("out_stored")

        block = st.enter_context(nc.Block())

        @block.sync
        def _(sp):
            sp.dma_start(w_raw[0][:, 0:KT, :], qkv_w[0, 0]).then_inc(w_in[0], 16)
            for k in range(0, KT, 2):
                sp.dma_start(x_raw[:, k, :], x_feat[:, k, :]).then_inc(x_in[k], 16)
            for w in (1, 2):
                sp.dma_start(w_raw[w][:, 0:KT, :], qkv_w[0, w]).then_inc(w_in[w], 16)

            def load_qkv(s):
                for w in range(2):
                    sp.wait_ge(w_mixed, 2 * (s - 1) + w + 1)
                    sp.dma_start(w_raw[w][:, 0:KT, :], qkv_w[s, w]).then_inc(w_in[w], 16)
                sp.wait_ge(w_rest, 3 * (s - 1) + 3)
                sp.dma_start(w_raw[2][:, :, :], qkv_w[s, 2]).then_inc(w_in[2], 16)

            load_qkv(1)
            for m, u in pairs_of_steps(sp, 1, PAIRS // 2):
                load_qkv(2 * m + u)

            def load_linear(t, u, weights, tile, kt):
                sp.wait_ge(lin_rest, t - 1)
                sp.dma_start(w_raw[u][:, 0:kt, :], weights[tile]).then_inc(lin_in[u], 16)

            for u in range(2):
                sp.wait_ge(w_mixed, 2 * PAIRS - 1 + u)
                sp.dma_start(w_raw[u][:, 0:KT, :], wo_w[u]).then_inc(lin_in[u], 16)
            sp.wait_ge(proj_done, 6 * PAIRS)
            sp.dma_start(resid[:, :, :, :], x_tok).then_inc(resid_in, 16)
            for u in range(2):
                load_linear(2 + u, u, wo_w, 2 + u, KT)

            def load_cf(b, c):
                if any_yet(2 * (b - 1) + c + 1):
                    sp.wait_ge(cf_rest, 2 * (b - 1) + c + 1)
                sp.dma_start(cf_raw[c][:, :, :],
                             ctx_feat[b, c]).then_inc(cf_in[c], 16)

            def load_ct(b, u):
                if any_yet(2 * (b - 2) + 2):
                    sp.wait_ge(cmixed, 2 * (b - 2) + 2)
                sp.dma_start(ct[u][:, :, :], ctx_tok[b]).then_inc(ct_in[u], 16)

            sp.wait_ge(heads_rest, 2 * PAIRS)
            load_cf(0, 0)
            load_cf(0, 1)
            load_ct(0, 0)
            for m, u in pairs_of_steps(sp, 2, KT // 2):
                load_linear(2 * m + u, u, wo_w, 2 * m + u, KT)
            load_ct(1, 1)
            for u in range(2):
                load_linear(8 + u, u, ffn_w, u, KT + 1)
            load_cf(1, 0)
            load_cf(1, 1)

            def load_context(b, u):
                load_cf(b, 0)
                load_cf(b, 1)
                load_ct(b, u)

            for m, u in pairs_of_steps(sp, 1, B // 2):
                load_context(2 * m + u, u)
            for m, u in pairs_of_steps(sp, 5, 8):
                load_linear(2 * m + u, u, ffn_w, 2 * m + u - 8, KT + 1)
            load_linear(16, 0, ffn_w, 8, KT + 1)
            for b in range(B):
                sp.wait_ge(out_ready, b + 1)
                sp.dma_start(out[b], resid[:, b, :, :]).then_inc(out_stored, 16)
            sp.wait_ge(out_stored, 16 * B)

        @block.tensor
        def _(pe):
            def project(s, w, h, first=False):
                if h == 0:
                    pe.wait_ge(w_rest, 3 * s + w + 1)
                if w == 0:
                    if any_yet(2 * (s - 1) + h + 1):
                        pe.wait_ge(v_kept, 2 * (s - 1) + h + 1)
                else:
                    pe.wait_ge(qk_kept, 4 * s + 2 * (w - 1) + h + 1)
                o = PROD[h][:, 0:HT]
                for k in range(KT):
                    if first:
                        pe.wait_ge(x_rest, k + 1)
                    for a, b in ((w_hi[w], x_hi), (w_hi[w], x_lo), (w_lo[w], x_hi)):
                        last = pe.matmul(o, a[:, k, :], b[:, k, HT * h:HT * h + HT],
                                         start=(k == 0 and b is x_hi and a is w_hi[w]),
                                         stop=(k == KT - 1 and a is w_lo[w]))
                last.then_inc(proj_done, 1)

            def turn_v(s, h):
                pe.wait_ge(v_kept, 2 * s + h + 1)
                if any_yet(4 * (s - 1) + 2 + h + 1):
                    pe.wait_ge(prob_t_kept, 4 * (s - 1) + 2 + h + 1)
                for b in range(HB):
                    last = pe.transpose(TURN[h][0:S, b * P:(b + 1) * P],
                                        v_feat[:, HB * h + b, :], ident[:, :])
                last.then_inc(v_turned, 1)

            def score(p, u, r):
                if r == 0:
                    pe.wait_ge(qk_kept, 4 * p + 4)
                if any_yet(4 * p + 2 * r):
                    pe.wait_ge(masked, 4 * p + 2 * r)
                for b in range(HB):
                    for h in range(2):
                        rows = slice(HD * h, HD * h + HD)
                        last = pe.matmul(SCORE[h][0:S, b * S:(b + 1) * S],
                                         qk[u][0][rows, HB * r + b, :],
                                         qk[u][1][rows, HB * r + b, :], start=True, stop=True)
                        if b == HB - 1:
                            last.then_inc(scored, 1)

            def turn_prob(p, r):
                for h in range(2):
                    a = 2 * r + h
                    pe.wait_ge(normed, 4 * p + a + 1)
                    if r == 0:
                        pe.wait_ge(v_tok_kept, 2 * p + h + 1)
                    else:
                        pe.wait_ge(prob_t_kept, 4 * p + h + 1)
                    for b in range(HB):
                        last = pe.transpose(TURN[h][0:S, b * S:(b + 1) * S],
                                            prob[a][:, b, :], ident[0:S, 0:S])
                    last.then_inc(prob_turned, 1)

            def mix_heads(p, r):
                pe.wait_ge(prob_t_kept, 4 * p + 2 * r + 2)
                pe.wait_ge(v_tok_kept, 2 * p + 2)
                if any_yet(2 * p + r):
                    pe.wait_ge(heads_rest, 2 * p + r)
                for b in range(HB):
                    for h in range(2):
                        last = pe.matmul(HEADS[HD * h:HD * h + HD, b * S:(b + 1) * S],
                                         v_tok[:, HB * r + b, HD * h:HD * h + HD],
                                         prob_t[2 * r + h][:, b, :], start=True, stop=True)
                last.then_inc(heads_done, 1)

            def attention_step(s, u, proj=True, attn=True):
                p, up = s - 1, 1 - u
                first = isinstance(s, int) and s == 0
                if proj:
                    project(s, 0, 0, first)
                if attn:
                    turn_v(p, 1)
                    score(p, up, 0)
                if proj:
                    project(s, 0, 1)
                if attn:
                    score(p, up, 1)
                if proj:
                    project(s, 1, 0)
                if attn:
                    turn_prob(p, 0)
                if proj:
                    project(s, 1, 1)
                if attn:
                    mix_heads(p, 0)
                    turn_prob(p, 1)
                if proj:
                    project(s, 2, 0)
                if attn:
                    mix_heads(p, 1)
                if proj:
                    project(s, 2, 1)
                    turn_v(s, 0)

            pe.wait_ge(const_in, 16 * 3)
            attention_step(0, 0, attn=False)
            attention_step(1, 1)
            for m, u in pairs_of_steps(pe, 1, PAIRS // 2):
                attention_step(2 * m + u, u)
            attention_step(PAIRS, 0, proj=False)

            def linear(t, u, h):
                if h == 0:
                    pe.wait_ge(lin_rest, t + 1)
                for k in range(KT):
                    for w, x in ((w_hi[u], act_hi), (w_hi[u], act_lo), (w_lo[u], act_hi)):
                        last = pe.matmul(PROD[h][:, 0:HT], w[:, k, :], x[:, k, HT * h:HT * h + HT],
                                         start=(k == 0 and w is w_hi[u] and x is act_hi),
                                         stop=(k == KT - 1 and w is w_lo[u]))
                last.then_inc(lin_done, 1)

            def turn_y(j, h):
                pe.wait_ge(y_kept, 2 * j + h + 1)
                if any_yet(2 * (j - 1) + h + 1):
                    pe.wait_ge(y_added, 2 * (j - 1) + h + 1)
                for b in range(HB):
                    last = pe.transpose(TURN[h][0:S, b * P:(b + 1) * P],
                                        y_feat[:, h, b * S:(b + 1) * S], ident[:, :])
                last.then_inc(y_turned, 1)

            def output_step(j, u, first=False):
                for h in range(2):
                    if h == 1 and not first:
                        turn_y(j - 1, 1)
                    if first:
                        pe.wait_ge(heads_rest, 2 * PAIRS - 1 + h)
                    if any_yet(2 * (j - 1) + h + 1):
                        pe.wait_ge(y_kept, 2 * (j - 1) + h + 1)
                    linear(j, u, h)
                turn_y(j, 0)

            output_step(0, 0, first=True)
            output_step(1, 1)
            for m, u in pairs_of_steps(pe, 1, KT // 2):
                output_step(2 * m + u, u)
            turn_y(KT - 1, 1)

            def turn_x1(b):
                pe.wait_ge(x1_ready, b + 1)
                if any_yet(2 * b):
                    pe.wait_ge(x1_rest, 2 * b)
                for c in range(2):
                    for k in range(4):
                        last = pe.transpose(TURN[c][:, k * S:(k + 1) * S], x1[:, 4 * c + k, :],
                                            ident[0:S, 0:S])
                    last.then_inc(x1_turned, 1)

            def cross_score(b):
                pe.wait_ge(x1_rest, 2 * b + 2)
                if any_yet(b):
                    pe.wait_ge(cexped, b)
                for c in range(2):
                    pe.wait_ge(cf_rest, 2 * b + c + 1)
                    for k in range(4 * c, 4 * c + 4):
                        for w, x in ((x1_hi, cf_hi), (x1_hi, cf_lo), (x1_lo, cf_hi)):
                            last = pe.matmul(SCORE[0][0:S, 0:LKP], w[:, k, :], x[:, k, :],
                                             start=(k == 0 and w is x1_hi and x is cf_hi),
                                             stop=(k == KT - 1 and w is x1_lo))
                    last.then_inc(cscored, 1)

            def turn_x2(b):
                pe.wait_ge(x2_ready, b + 1)
                pe.wait_ge(x2_rest, 2 * b)
                for c in range(2):
                    for k in range(4):
                        last = pe.transpose(X2T[c][:, k * S:(k + 1) * S], x2[:, 4 * c + k, :],
                                            ident[0:S, 0:S])
                    last.then_inc(x2_turned, 1)

            def cross_mix(b, u, m):
                pe.wait_ge(cprob_t_kept, b + 1)
                pe.wait_ge(ct_in[u], 16 * m + 16)
                if any_yet(2 * b):
                    pe.wait_ge(cadded, 2 * b)
                for n in range(2):
                    for c in range(CC):
                        last = pe.matmul(PROD[n][0:S, :], cprob_t[:, c, :],
                                         ct[u][:, c, 512 * n:512 * n + 512],
                                         start=(c == 0), stop=(c == CC - 1))
                    last.then_inc(cmixed, 1)

            def turn_cprob(b):
                pe.wait_ge(cnormed, b + 1)
                if any_yet(b):
                    pe.wait_ge(cprob_t_kept, b)
                for c in range(CC):
                    last = pe.transpose(HEADS[0:CR, c * S:(c + 1) * S],
                                        cprob[:, c * CR:(c + 1) * CR], ident[0:S, 0:S])
                last.then_inc(cturned, 1)

            def cross_step(b, u, m):
                known = isinstance(b, int)
                if not known or b < B:
                    cross_score(b)
                if not known or b >= 2:
                    turn_x2(b - 2)
                if not known or b + 1 < B:
                    turn_x1(b + 1)
                if not known or 1 <= b <= B:
                    cross_mix(b - 1, 1 - u, m - 1 if u == 0 else m)
                if not known or b < B:
                    turn_cprob(b)

            pe.wait_ge(y_kept, 2 * KT)
            turn_x1(0)
            cross_step(0, 0, 0)
            cross_step(1, 1, 0)
            for m, u in pairs_of_steps(pe, 1, 3):
                cross_step(2 * m + u, u, m)
            for b in range(6, B + 2):
                cross_step(b, b % 2, b // 2)

            def lora(h):
                if h == 0:
                    pe.wait_ge(cadded, 2 * B)
                pe.wait_ge(x2_rest, 2 * HB * (h + 1))
                linear(8, 0, h)

            def ffn_product(j, t, u, h, first=False):
                if h == 0:
                    pe.wait_ge(lin_rest, t + 1)
                if first:
                    pe.wait_ge(t_masked, h + 1)
                else:
                    pe.wait_ge(y_kept, 2 * (KT + j - 1) + h + 1)
                for k in range(KT + 1):
                    w = (w_hi[u][:, k, :], w_lo[u][:, k, :])
                    x = (act_hi[:, k % KT, HT * h:HT * h + HT], act_lo[:, k % KT, HT * h:HT * h + HT])
                    if k == KT:
                        if first:
                            pe.wait_ge(t_rest, h + 1)
                        w = (w_hi[u][0:EXTRA, k, :], w_lo[u][0:EXTRA, k, :])
                        x = (t_hi[:, HB * h:HB * h + HB, :], t_lo[:, HB * h:HB * h + HB, :])
                    for a, b in ((0, 0), (0, 1), (1, 0)):
                        last = pe.matmul(PROD[h][:, 0:HT], w[a], x[b],
                                         start=(k == 0 and (a, b) == (0, 0)),
                                         stop=(k == KT and a == 1))
                last.then_inc(lin_done, 1)

            def ffn_step(j, t, u, first=False):
                for h in range(2):
                    if h == 1 and not first:
                        turn_y(KT + j - 1, 1)
                    if first:
                        lora(h)
                    ffn_product(j, t, u, h, first)
                turn_y(KT + j, 0)

            ffn_step(0, 9, 1, first=True)
            for m, u in pairs_of_steps(pe, 5, 8):
                ffn_step(2 * m + u - 9, 2 * m + u, u)
            ffn_step(7, 16, 0)
            turn_y(2 * KT - 1, 1)

        @block.scalar
        def _(act):
            for k in range(1, KT, 2):
                act.dma_start(x_raw[:, k, :], x_feat[:, k, :]).then_inc(x_in[k], 16)
            act.dma_start(ident[:, :], identity).then_inc(const_in, 16)
            act.dma_start(turn[:, :], rotary).then_inc(const_in, 16)
            act.dma_start(mask[:, :], causal).then_inc(const_in, 16)
            act.dma_start(route_c[:, :], route).then_inc(const_in, 16)
            act.dma_start(starts_i[:, :], starts).then_inc(const_in, 16)

            def round_w(s, w):
                if w < 2:
                    act.wait_ge(w_mixed, 2 * s + w + 1)
                else:
                    act.wait_ge(w_in[2], 16 * s + 16)
                if any_yet(6 * (s - 1) + 2 * w + 2):
                    act.wait_ge(proj_done, 6 * (s - 1) + 2 * w + 2)
                src = w_mix if w < 2 else w_raw[2]
                act.activation(w_hi[w][:, 0:KT, :], src[:, 0:KT, :], ACT.Copy).then_inc(w_rounded, 1)

            def keep_v(s, h):
                act.wait_ge(proj_done, 6 * s + 4 + h + 1)
                if any_yet(2 * (s - 1) + h + 1):
                    act.wait_ge(v_turned, 2 * (s - 1) + h + 1)
                act.activation(v_feat[:, HB * h:HB * h + HB, :], PROD[h][:, 0:HT],
                               ACT.Copy).then_inc(v_kept, 1)

            def keep_v_tok(s, h):
                act.wait_ge(v_turned, 2 * s + h + 1)
                act.activation(v_tok[:, HB * h:HB * h + HB, :], TURN[h][0:S, :],
                               ACT.Copy).then_inc(v_tok_kept, 1)

            def exponentials(p, r):
                for h in range(2):
                    a = 2 * r + h
                    act.wait_ge(shifted, 4 * p + a + 1)
                    for b in range(HB):
                        last = act.activation(prob[a][:, b, :], prob[a][:, b, :], ACT.Exp,
                                              bias=shift[:, a, b:b + 1], scale=SCORE_SCALE,
                                              accum_out=total[:, a, b:b + 1])
                    last.then_inc(exped, 1)

            def keep_prob_t(p, r):
                for h in range(2):
                    a = 2 * r + h
                    act.wait_ge(prob_turned, 4 * p + a + 1)
                    if any_yet(2 * (p - 1) + r + 1):
                        act.wait_ge(heads_done, 2 * (p - 1) + r + 1)
                    act.activation(prob_t[a][:, :, :], TURN[h][0:S, 0:HT],
                                   ACT.Copy).then_inc(prob_t_kept, 1)

            def round_heads(p, r):
                act.wait_ge(heads_done, 2 * p + r + 1)
                act.activation(act_hi[:, p, HT * r:HT * r + HT], HEADS[:, 0:HT],
                               ACT.Copy).then_inc(heads_rounded, 1)

            def attention_step(s, proj=True, attn=True, prepare=True):
                p = s - 1
                if proj:
                    round_w(s, 2)
                if attn:
                    keep_v_tok(p, 1)
                    exponentials(p, 0)
                if prepare:
                    round_w(s + 1, 0)
                if attn:
                    exponentials(p, 1)
                    keep_prob_t(p, 0)
                if prepare:
                    round_w(s + 1, 1)
                if attn:
                    round_heads(p, 0)
                    keep_prob_t(p, 1)
                if proj:
                    keep_v(s, 0)
                if attn:
                    round_heads(p, 1)
                if proj:
                    keep_v(s, 1)
                    keep_v_tok(s, 0)

            def round_linear(t, u, kt, half_uses):
                act.wait_ge(lin_in[u], 16 * half_uses + 16)
                if any_yet(2 * (t - 2) + 2):
                    act.wait_ge(lin_done, 2 * (t - 2) + 2)
                act.activation(w_hi[u][:, 0:kt, :], w_raw[u][:, 0:kt, :],
                               ACT.Copy).then_inc(lin_rounded, 1)

            for w in range(2):
                if w == 0:
                    round_w(0, 0)
                    for k in range(KT):
                        act.wait_ge(x_in[k], 16)
                        act.activation(x_hi[:, k, :], x_raw[:, k, :], ACT.Copy).then_inc(x_rounded, 1)
                else:
                    round_w(0, 1)
            attention_step(0, attn=False)
            attention_step(1)
            for m, u in pairs_of_steps(act, 1, PAIRS // 2 - 1):
                attention_step(2 * m + u)
            attention_step(PAIRS - 2)
            attention_step(PAIRS - 1, prepare=False)
            act.wait_ge(proj_done, 6 * PAIRS)
            round_linear(0, 0, KT, 0)
            round_linear(1, 1, KT, 0)
            attention_step(PAIRS, proj=False, prepare=False)

            def keep_y(j, n, h):
                act.wait_ge(lin_done, n + h + 1)
                if any_yet(2 * (j - 1) + h + 1):
                    act.wait_ge(y_turned, 2 * (j - 1) + h + 1)
                act.activation(y_feat[:, h, :], PROD[h][:, 0:HT], ACT.Copy).then_inc(y_kept, 1)

            def output_step(j):
                keep_y(j, 2 * j, 0)
                keep_y(j, 2 * j, 1)

            output_step(0)
            round_linear(2, 0, KT, 1)
            output_step(1)
            round_linear(3, 1, KT, 1)
            for m, u in pairs_of_steps(act, 1, KT // 2 - 1):
                output_step(2 * m + u)
                round_linear(2 * m + u + 2, u, KT, m + 1)
            output_step(KT - 2)
            output_step(KT - 1)

            def round_cf(b, c):
                act.wait_ge(cf_in[c], 16 * b + 16)
                if any_yet(2 * (b - 1) + c + 1):
                    act.wait_ge(cscored, 2 * (b - 1) + c + 1)
                act.activation(cf_hi[:, 4 * c:4 * c + 4, :], cf_raw[c][:, :, :],
                               ACT.Copy).then_inc(cf_rounded, 1)

            def keep_x1(b):
                act.wait_ge(x1_ready, b + 1)
                act.activation(resid[:, b, :, :], x1[:, :, :], ACT.Copy).then_inc(x1_kept, 1)

            def round_x1(b):
                for c in range(2):
                    act.wait_ge(x1_turned, 2 * b + c + 1)
                    if any_yet(2 * b):
                        act.wait_ge(cscored, 2 * b)
                    act.activation(x1_hi[:, 4 * c:4 * c + 4, :], TURN[c][:, 0:4 * S],
                                   ACT.Copy).then_inc(x1_rounded, 1)

            def round_x2(b):
                for c in range(2):
                    act.wait_ge(x2_turned, 2 * b + c + 1)
                    act.activation(by_row(act_hi)[:, 4 * c:4 * c + 4, b, :], X2T[c][:, 0:4 * S],
                                   ACT.Copy).then_inc(x2_rounded, 1)

            def by_row(t):
                return t[:, :, :].rearrange("p k (b s) -> p k b s", b=B)

            def cross_step(b):
                known = isinstance(b, int)
                if not known or b + 1 < B:
                    round_cf(b + 1, 0)
                if not known or b >= 2:
                    act.wait_ge(cvar, b - 1)
                    act.activation(mv2[:, 2:3], mv2[:, 1:2], ACT.Sqrt).then_inc(cstd, 1)
                if not known or b < B:
                    act.wait_ge(cshifted, b + 1)
                    act.activation(cprob[:, 0:LK], SCORE[0][0:S, 0:LK], ACT.Exp,
                                   bias=ctop[:, 1:2], accum_out=ctop[:, 2:3]).then_inc(cexped, 1)
                if not known or b >= 2:
                    round_x2(b - 2)
                if not known or b + 1 < B:
                    round_x1(b + 1)
                if not known or b >= 2:
                    act.wait_ge(x2_ready, b - 1)
                    act.activation(resid[:, b - 2, :, :], x2[:, :, :], ACT.Copy).then_inc(x2_kept, 1)
                if not known or b + 1 < B:
                    round_cf(b + 1, 1)
                if not known or b + 2 < B:
                    keep_x1(b + 2)
                if not known or b < B:
                    act.wait_ge(cturned, b + 1)
                    if any_yet(2 * b):
                        act.wait_ge(cmixed, 2 * b)
                    act.activation(cprob_t[:, :, :], HEADS[0:CR, 0:CC * S],
                                   ACT.Copy).then_inc(cprob_t_kept, 1)

            act.wait_ge(heads_rest, 2 * PAIRS)
            round_cf(0, 0)
            round_cf(0, 1)
            act.wait_ge(norm_var, 1)
            act.activation(rstd[:, :, 0], rstd[:, :, 0], ACT.Sqrt).then_inc(norm_std, 1)
            keep_x1(0)
            round_x1(0)
            keep_x1(1)
            cross_step(0)
            round_linear(8, 0, KT + 1, 4)
            round_linear(9, 1, KT + 1, 4)
            cross_step(1)
            for m, u in pairs_of_steps(act, 1, 3):
                cross_step(2 * m + u)
            for b in range(6, B + 2):
                cross_step(b)

            def round_t(h):
                act.wait_ge(t_masked, h + 1)
                act.wait_ge(t_filled, 1)
                act.activation(t_hi[0:RA, HB * h:HB * h + HB, :], t_raw[:, HB * h:HB * h + HB, :],
                               ACT.Copy).then_inc(t_rounded, 1)

            round_t(0)
            act.wait_ge(lin_done, 2 * KT + 2)
            act.activation(y_feat[:, 0, :], PROD[0][:, 0:HT], ACT.Copy).then_inc(y_kept, 1)
            round_t(1)
            act.wait_ge(lin_done, 2 * KT + 4)
            act.activation(y_feat[:, 1, :], PROD[1][:, 0:HT], ACT.Copy).then_inc(y_kept, 1)
            round_linear(10, 0, KT + 1, 5)
            round_linear(11, 1, KT + 1, 5)
            for m, u in pairs_of_steps(act, 5, 7):
                j = 2 * m + u - 9
                keep_y(KT + j, 2 * (2 * m + u), 0)
                keep_y(KT + j, 2 * (2 * m + u), 1)
                round_linear(2 * m + u + 2, u, KT + 1, m + 1)
            for t in range(14, 17):
                keep_y(KT + t - 9, 2 * t, 0)
                keep_y(KT + t - 9, 2 * t, 1)
                if t == 14:
                    round_linear(16, 0, KT + 1, 8)
            act.wait_ge(norm_var, 2)
            act.activation(rstd[:, :, 0], rstd[:, :, 0], ACT.Sqrt).then_inc(norm_std, 1)

        @block.vector
        def _(dve):
            dve.wait_ge(const_in, 16 * 5)
            dve.tensor_copy(starts_f[:, :], starts_i[:, :]).then_inc(routed, 1)
            dve.wait_ge(routed, 1)
            for i in range(NA + 1):
                dve.tensor_scalar(passed[:, i, :], route_c[:, 0:B], starts_f[:, i:i + 1], None,
                                  ALU.is_ge).then_inc(routed, 1)
            for i in range(1, NA + 1):
                dve.wait_ge(routed, 4 + i)
                dve.tensor_tensor(passed[:, 0, :], passed[:, 0, :], passed[:, i, :],
                                  ALU.add).then_inc(routed, 1)
            dve.wait_ge(routed, 5 + NA)
            dve.tensor_scalar(sel[:, :], passed[:, 0, :], route_c[:, B:B + 1], None,
                              ALU.is_equal).then_inc(routed, 1)

            for k in range(KT):
                dve.wait_ge(x_rounded, k + 1)
                dve.tensor_tensor(x_lo[:, k, :], x_raw[:, k, :], x_hi[:, k, :].bitcast(F32),
                                  ALU.subtract).then_inc(x_rest, 1)

            scale = turn[:, :].unsqueeze(1).broadcast_to([P, HB, S])
            hidden = mask[:, :].unsqueeze(1).broadcast_to([S, HB, S])

            def keep_qk(s, u, w, h):
                dve.wait_ge(proj_done, 6 * s + 2 * w + h + 1)
                if w == 0 and h == 0:
                    if any_yet(4 * (s - 1)):
                        dve.wait_ge(scored, 4 * (s - 1))
                dve.tensor_tensor(qk[u][w][:, HB * h:HB * h + HB, :],
                                  PROD[h][:, 0:HT].rearrange("p (b s) -> p b s", b=HB),
                                  scale, ALU.mult).then_inc(qk_kept, 1)

            def mask_and_top(p, r):
                for h in range(2):
                    a = 2 * r + h
                    dve.wait_ge(scored, 4 * p + a + 1)
                    if any_yet(4 * (p - 1) + a + 1):
                        dve.wait_ge(prob_turned, 4 * (p - 1) + a + 1)
                    dve.tensor_tensor(prob[a][:, :, :],
                                      SCORE[h][0:S, 0:HT].rearrange("p (b s) -> p b s", b=HB),
                                      hidden, ALU.add).then_inc(masked, 1)
                for h in range(2):
                    a = 2 * r + h
                    dve.wait_ge(masked, 4 * p + a + 1)
                    dve.tensor_reduce(top[:, a, :], prob[a][:, :, :], AX.X,
                                      ALU.max).then_inc(topped, 1)
                for h in range(2):
                    a = 2 * r + h
                    dve.wait_ge(topped, 4 * p + a + 1)
                    dve.tensor_scalar(shift[:, a, :], top[:, a, :], -SCORE_SCALE, None,
                                      ALU.mult).then_inc(shifted, 1)

            def normalise(p, r):
                for h in range(2):
                    a = 2 * r + h
                    dve.wait_ge(exped, 4 * p + a + 1)
                    dve.reciprocal(inv[:, a, :], total[:, a, :]).then_inc(inverted, 1)
                for h in range(2):
                    a = 2 * r + h
                    dve.wait_ge(inverted, 4 * p + a + 1)
                    dve.tensor_tensor(prob[a][:, :, :], prob[a][:, :, :],
                                      inv[:, a, :].unsqueeze(2).broadcast_to([S, HB, S]),
                                      ALU.mult).then_inc(normed, 1)

            def rest_heads(p, r):
                dve.wait_ge(heads_rounded, 2 * p + r + 1)
                dve.tensor_tensor(act_lo[:, p, HT * r:HT * r + HT], HEADS[:, 0:HT],
                                  act_hi[:, p, HT * r:HT * r + HT].bitcast(F32),
                                  ALU.subtract).then_inc(heads_rest, 1)

            def attention_step(s, u, proj=True, attn=True):
                p = s - 1
                if proj:
                    keep_qk(s, u, 0, 0)
                if attn:
                    mask_and_top(p, 0)
                if proj:
                    keep_qk(s, u, 0, 1)
                if attn:
                    normalise(p, 0)
                    mask_and_top(p, 1)
                if proj:
                    keep_qk(s, u, 1, 0)
                if attn:
                    normalise(p, 1)
                if proj:
                    keep_qk(s, u, 1, 1)
                if attn:
                    rest_heads(p, 0)
                    rest_heads(p, 1)

            attention_step(0, 0, attn=False)
            attention_step(1, 1)
            for m, u in pairs_of_steps(dve, 1, PAIRS // 2):
                attention_step(2 * m + u, u)
            attention_step(PAIRS, 0, proj=False)

            def add_y(j, n, first=False):
                for h in range(2):
                    rows = slice(HB * h, HB * h + HB)
                    dve.wait_ge(y_turned, 2 * n + h + 1)
                    if first:
                        dve.wait_ge(resid_in, 16)
                    dve.tensor_tensor(resid[:, rows, j, :],
                                      TURN[h][0:S, :].rearrange("p (b s) -> p b s", b=HB),
                                      resid[:, rows, j, :], ALU.add).then_inc(y_added, 1)
                    dve.wait_ge(y_added, 2 * n + h + 1)
                    for b in range(HB * h, HB * h + HB):
                        last = dve.bn_stats(stats[:, b, j, :], resid[:, b, j, :])
                last.then_inc(y_stats, 1)

            def row_norms(n):
                dve.wait_ge(y_stats, 8 * n)
                for b in range(B):
                    last = dve.bn_aggr(mv[:, b, :], stats[:, b, :, :])
                last.then_inc(norm_aggr, 1)
                dve.wait_ge(norm_aggr, n)
                dve.tensor_scalar(rstd[:, :, 0], mv[:, :, 1], EPS, None, ALU.add).then_inc(norm_var, 1)
                dve.wait_ge(norm_std, n)
                dve.reciprocal(rstd[:, :, 0], rstd[:, :, 0]).then_inc(norm_inv, 1)
                dve.wait_ge(norm_inv, n)

            add_y(0, 0, first=True)
            add_y(1, 1)
            for m, u in pairs_of_steps(dve, 1, KT // 2):
                add_y(2 * m + u, 2 * m + u)
            row_norms(1)

            def norm_x1(b):
                if any_yet(2 * b):
                    dve.wait_ge(x1_turned, 2 * b)
                if any_yet(b):
                    dve.wait_ge(x1_kept, b)
                dve.tensor_scalar(x1[:, :, :], resid[:, b, :, :], mv[:, b, 0:1], rstd[:, b, :],
                                  ALU.subtract, ALU.mult).then_inc(x1_ready, 1)

            def rest_x1(b):
                for c in range(2):
                    dve.wait_ge(x1_rounded, 2 * b + c + 1)
                    dve.tensor_tensor(x1_lo[:, 4 * c:4 * c + 4, :],
                                      TURN[c][:, 0:4 * S].rearrange("p (k s) -> p k s", k=4),
                                      x1_hi[:, 4 * c:4 * c + 4, :].bitcast(F32),
                                      ALU.subtract).then_inc(x1_rest, 1)

            def rest_x2(b):
                for c in range(2):
                    ks = slice(4 * c, 4 * c + 4)
                    dve.wait_ge(x2_rounded, 2 * b + c + 1)
                    dve.tensor_tensor(act_lo[:, :, :].rearrange("p k (b s) -> p k b s", b=B)[:, ks, b, :],
                                      X2T[c][:, 0:4 * S].rearrange("p (k s) -> p k s", k=4),
                                      act_hi[:, :, :].bitcast(F32)
                                      .rearrange("p k (b s) -> p k b s", b=B)[:, ks, b, :],
                                      ALU.subtract).then_inc(x2_rest, 1)

            def norm_x2(b):
                dve.wait_ge(x2_turned, 2 * b)
                dve.wait_ge(x2_kept, b)
                for n in range(2):
                    ks = slice(4 * n, 4 * n + 4)
                    dve.wait_ge(cmixed, 2 * b + n + 1)
                    dve.wait_ge(x1_kept, b + 1)
                    dve.tensor_tensor(x2[:, ks, :],
                                      PROD[n][0:S, :].rearrange("p (k s) -> p k s", k=4),
                                      resid[:, b, ks, :], ALU.add).then_inc(cadded, 1)
                for n in range(2):
                    dve.wait_ge(cadded, 2 * b + n + 1)
                    last = dve.bn_stats(stats2[:, n, :], x2[:, 4 * n:4 * n + 4, :])
                last.then_inc(cstats, 1)
                dve.wait_ge(const_in, 16 * 5)
                dve.wait_ge(cstats, b + 1)
                dve.bn_aggr(mv2[:, 0:2], stats2[:, :, :]).then_inc(caggr, 1)
                dve.wait_ge(caggr, b + 1)
                dve.tensor_scalar(mv2[:, 1:2], mv2[:, 1:2], EPS, None, ALU.add).then_inc(cvar, 1)
                dve.wait_ge(cstd, b + 1)
                dve.reciprocal(mv2[:, 3:4], mv2[:, 2:3]).then_inc(cinv, 1)
                dve.wait_ge(cinv, b + 1)
                dve.tensor_scalar(x2[:, :, :], x2[:, :, :], mv2[:, 0:1], mv2[:, 3:4],
                                  ALU.subtract, ALU.mult).then_inc(x2_ready, 1)

            def cross_step(b):
                known = isinstance(b, int)
                if not known or b >= 2:
                    norm_x2(b - 2)
                if not known or b < B:
                    dve.wait_ge(cscored, 2 * b + 2)
                    if any_yet(b):
                        dve.wait_ge(cturned, b)
                    dve.tensor_reduce(ctop[:, 0:1], SCORE[0][0:S, 0:LK], AX.X,
                                      ALU.max).then_inc(ctopped, 1)
                    dve.wait_ge(ctopped, b + 1)
                    dve.tensor_scalar(ctop[:, 1:2], ctop[:, 0:1], -1.0, None,
                                      ALU.mult).then_inc(cshifted, 1)
                if not known or b >= 2:
                    rest_x2(b - 2)
                if not known or b + 1 < B:
                    rest_x1(b + 1)
                if not known or b < B:
                    dve.wait_ge(cexped, b + 1)
                    dve.reciprocal(ctop[:, 3:4], ctop[:, 2:3]).then_inc(cinverted, 1)
                    dve.wait_ge(cinverted, b + 1)
                    dve.tensor_scalar(cprob[:, 0:LK], cprob[:, 0:LK], ctop[:, 3:4], None,
                                      ALU.mult).then_inc(cnormed, 1)
                if not known or b + 2 < B:
                    norm_x1(b + 2)

            norm_x1(0)
            rest_x1(0)
            norm_x1(1)
            cross_step(0)
            cross_step(1)
            for m, u in pairs_of_steps(dve, 1, 3):
                cross_step(2 * m + u)
            for b in range(6, B + 2):
                cross_step(b)

            dve.memset(t_hi[32:EXTRA, :, :].bitcast(F32), 1.0)
            dve.memset(t_lo[:, :, :].bitcast(F32), 0.0).then_inc(t_filled, 1)

            def mask_t(h):
                rows = slice(HB * h, HB * h + HB)
                dve.wait_ge(lin_done, 2 * KT + 2 * h + 1)
                dve.tensor_tensor(t_raw[:, rows, :],
                                  PROD[h][0:RA, 0:HT].rearrange("p (b s) -> p b s", b=HB),
                                  sel[:, rows].unsqueeze(2).broadcast_to([RA, HB, S]),
                                  ALU.mult).then_inc(t_masked, 1)
                dve.wait_ge(t_rounded, h + 1)
                dve.tensor_tensor(t_lo[0:RA, rows, :], t_raw[:, rows, :],
                                  t_hi[0:RA, rows, :].bitcast(F32), ALU.subtract).then_inc(t_rest, 1)

            dve.wait_ge(t_filled, 1)
            mask_t(0)
            mask_t(1)
            add_y(0, KT)
            for m, u in pairs_of_steps(dve, 5, 8):
                add_y(2 * m + u - 9, KT + 2 * m + u - 9)
            add_y(7, 2 * KT - 1)
            row_norms(2)
            for b in range(B):
                dve.tensor_scalar(resid[:, b, :, :], resid[:, b, :, :], mv[:, b, 0:1],
                                  rstd[:, b, :], ALU.subtract, ALU.mult).then_inc(out_ready, 1)

        @block.gpsimd
        def _(pool):
            def prepare_w(s):
                for w in range(2):
                    pool.wait_ge(w_in[w], 16 * s + 16)
                    if w == 0:
                        if any_yet(3 * s - 1):
                            pool.wait_ge(w_rest, 3 * s - 1)
                    else:
                        pool.wait_ge(w_rest, 3 * s + 1)
                    raw = w_raw[w][:, 0:KT, :].rearrange("p k (h t i) -> p (k h) t i", h=2, t=2)
                    mix = w_mix[:, :, :].rearrange("p k (h t i) -> p (k h) t i", h=2, t=2)
                    pool.tensor_tensor(mix[:, :, 0, :], raw[:, :, 0, :], raw[:, :, 1, :], ALU.add)
                    pool.tensor_tensor(mix[:, :, 1, :], raw[:, :, 0, :], raw[:, :, 1, :],
                                       ALU.subtract).then_inc(w_mixed, 1)
                    pool.wait_ge(w_rounded, 3 * s + w + 1)
                    pool.tensor_tensor(w_lo[w][:, 0:KT, :], w_mix[:, :, :],
                                       w_hi[w][:, 0:KT, :].bitcast(F32),
                                       ALU.subtract).then_inc(w_rest, 1)
                pool.wait_ge(w_rounded, 3 * s + 3)
                pool.tensor_tensor(w_lo[2][:, :, :], w_raw[2][:, :, :],
                                   w_hi[2][:, :, :].bitcast(F32), ALU.subtract).then_inc(w_rest, 1)

            prepare_w(0)
            prepare_w(1)
            for m, u in pairs_of_steps(pool, 1, PAIRS // 2):
                prepare_w(2 * m + u)

            def rest_linear(t, u, kt):
                pool.wait_ge(lin_rounded, t + 1)
                pool.tensor_tensor(w_lo[u][:, 0:kt, :], w_raw[u][:, 0:kt, :],
                                   w_hi[u][:, 0:kt, :].bitcast(F32),
                                   ALU.subtract).then_inc(lin_rest, 1)

            rest_linear(0, 0, KT)
            rest_linear(1, 1, KT)
            for m, u in pairs_of_steps(pool, 1, KT // 2):
                rest_linear(2 * m + u, u, KT)

            def rest_cf(b):
                for c in range(2):
                    pool.wait_ge(cf_rounded, 2 * b + c + 1)
                    pool.tensor_tensor(cf_lo[:, 4 * c:4 * c + 4, :], cf_raw[c][:, :, :],
                                       cf_hi[:, 4 * c:4 * c + 4, :].bitcast(F32),
                                       ALU.subtract).then_inc(cf_rest, 1)

            rest_cf(0)
            rest_cf(1)
            rest_linear(8, 0, KT + 1)
            rest_linear(9, 1, KT + 1)
            for m, u in pairs_of_steps(pool, 1, B // 2):
                rest_cf(2 * m + u)
            for m, u in pairs_of_steps(pool, 5, 8):
                rest_linear(2 * m + u, u, KT + 1)
            rest_linear(16, 0, KT + 1)


def constants():
    freq = (1.0 / 10000.0 ** (np.arange(0, HD, 2, dtype=np.float32) / np.float32(HD))).astype(np.float32)
    angle = np.arange(S, dtype=np.float32)[None, :] * freq[:, None]
    sin, cos = np.sin(angle), np.cos(angle)
    rotary = np.concatenate([cos + sin, cos - sin] * 2, 0).astype(np.float32)
    causal = np.where(np.tril(np.ones((S, S), bool)), 0.0, MASKED).astype(np.float32)
    route = np.empty((RA, B + 1), np.float32)
    route[:, :B] = np.arange(B)
    route[:, B] = np.arange(RA) // R + 2
    return {"rotary": rotary, "causal": causal, "identity": np.eye(P, dtype=np.float32), "route": route}


def tiles(w):
    return w.reshape(KT, P, KT, P).transpose(2, 1, 0, 3)


def kernel(**inputs):
    import concourse.bacc as bacc
    from concourse.bass_utils import run_bass_kernel_spmd as run

    a = {k: np.asarray(v) for k, v in inputs.items()}
    x, ctx = a["x"], a["ctx_4096"]
    order = np.arange(D).reshape(D // HD, HD // 2, 2).transpose(0, 2, 1).reshape(-1)
    qkv = np.stack([tiles(a["L0_attn_Wq"][:, order]), tiles(a["L0_attn_Wk"][:, order]),
                    tiles(a["L0_attn_Wv"])], 1)
    ffn = np.zeros((KT + 1, P, KT + 1, P), np.float32)
    ffn[0, :, :KT, :RA] = a["L0_ffn_lora_A"].reshape(RA, KT, P).transpose(2, 1, 0)
    ffn[1:, :, :KT, :] = tiles(a["L0_ffn_weight"].T)
    ffn[1:, :RA, KT, :] = a["L0_ffn_lora_B"].transpose(0, 2, 1).reshape(RA, KT, P).transpose(1, 0, 2)
    ffn[1:, BIAS_ROW, KT, :] = a["L0_ffn_bias"].reshape(KT, P)
    ctx_feat = np.zeros((B, 2, P, KT // 2, LKP), np.float32)
    ctx_feat[..., :LK] = ctx.transpose(0, 2, 1).reshape(B, 2, KT // 2, P, LK).transpose(0, 1, 3, 2, 4)
    starts = a["L0_ffn_lora_start_indices"]
    arrays = {
        "x_feat": x.reshape(B * S, KT, P).transpose(2, 1, 0),
        "x_tok": x.transpose(1, 0, 2).reshape(S, B, KT, P),
        "qkv_w": qkv,
        "wo_w": tiles(a["L0_attn_Wo"]),
        "ffn_w": ffn,
        "ctx_feat": ctx_feat,
        "ctx_tok": ctx.reshape(B, CC, CR, D).transpose(0, 2, 1, 3),
        "starts": np.broadcast_to(starts[None, :], (RA, NA + 1)),
        **constants(),
    }
    arrays = {k: np.ascontiguousarray(v) for k, v in arrays.items()}
    nc = bacc.Bacc("TRN2", target_bir_lowering=False, num_devices=1)
    args = {k: nc.dram_tensor(k, v.shape, mybir.dt.from_np(v.dtype), kind="ExternalInput").ap()
            for k, v in arrays.items()}
    out = nc.dram_tensor("out", (B, S, D), F32, kind="ExternalOutput").ap()
    build(nc, out=out.rearrange("b s (k f) -> b s k f", k=KT), **args)
    r = run(nc, [arrays], core_ids=[0])
    return r.results[0]["out"]
```

```python
from contextlib import ExitStack

import numpy as np

import concourse.bass as bass
from concourse import mybir

F32 = mybir.dt.float32
F32R = mybir.dt.float32r
I32 = mybir.dt.int32
ALU = mybir.AluOpType
ACT = mybir.ActivationFunctionType
AX = mybir.AxisListType

P = 128
B = 8
S = 112
D = 1024
KT = D // P
HD = 64
PAIRS = D // (2 * HD)
HB = B // 2
HT = HB * S
LK = 375
LKP = LK + 1
CR = 125
CC = LK // CR
R = 16
NA = 3
RA = NA * R
BIAS_ROW = RA
EXTRA = 64
EPS = 1e-5
MASKED = -2e9
SCORE_SCALE = 1.0 / (2.0 * HD ** 0.5)


def any_yet(n):
    return not isinstance(n, int) or n > 0


def pairs_of_steps(eng, first, last):
    with eng.Fori(first, last) as m:
        yield m, 0
        yield m, 1


def build(nc, x_feat, x_tok, qkv_w, wo_w, ffn_w, ctx_feat, ctx_tok, starts, rotary, causal,
          identity, route, out):
    st = ExitStack()
    with st:
        def sb(name, shape, dt=F32, scope=st):
            return scope.enter_context(nc.sbuf_tensor(name, shape, dt))

        def sem(name):
            return st.enter_context(nc.semaphore(name))

        with ExitStack() as early:
            x_raw = sb("x_raw", [P, KT, B * S], F32, early)
            w_mix0 = sb("w_mix0", [P, KT, P], F32, early)
        act_hi = sb("act_hi", [P, KT, B * S], F32R)
        act_lo = sb("act_lo", [P, KT, B * S], F32R)
        w_raw = [sb(f"w_raw{i}", [P, KT + 1, P]) for i in range(2)]
        w_hi = [sb(f"w_hi{i}", [P, KT + 1, P], F32R) for i in range(2)]
        w_lo = [sb(f"w_lo{i}", [P, KT + 1, P], F32R) for i in range(2)]
        y_feat = sb("y_feat", [P, 2, HT])
        ident = sb("ident", [P, P])
        mask = sb("mask", [S, S])
        turn = sb("turn", [P, S])
        stats = sb("stats", [S, B, KT, 6])
        mv = sb("mv", [S, B, 2])
        var_eps = sb("var_eps", [S, B])
        rstd = sb("rstd", [S, B, 1])
        centre = sb("centre", [S, B, 1])
        minus_half = sb("minus_half", [S, HB])
        route_c = sb("route_c", [RA, B + 1])
        starts_i = sb("starts_i", [RA, NA + 1], I32)
        starts_f = sb("starts_f", [RA, NA + 1])
        passed = sb("passed", [RA, NA + 1, B])
        sel = sb("sel", [RA, B])
        with ExitStack() as one:
            x_hi = sb("x_hi", [P, KT, B * S], F32R, one)
            x_lo = sb("x_lo", [P, KT, B * S], F32R, one)
            w_raw.append(sb("w_raw2", [P, KT, P], F32, one))
            w_hi.append(sb("w_hi2", [P, KT, P], F32R, one))
            w_lo.append(sb("w_lo2", [P, KT, P], F32R, one))
            w_mix = sb("w_mix", [P, KT, P], F32, one)
            qk = [[sb(f"{n}{i}", [P, B, S], F32, one) for n in ("q_feat", "k_feat")]
                  for i in range(2)]
            v_feat = sb("v_feat", [P, B, S], F32, one)
            v_tok = sb("v_tok", [S, B, P], F32, one)
            prob = [sb(f"prob{i}", [S, HB, S], F32, one) for i in range(4)]
            prob_t = [sb(f"prob_t{i}", [S, HB, S], F32, one) for i in range(4)]
            top = sb("top", [S, 4, HB], F32, one)
            shift = sb("shift", [S, 4, HB], F32, one)
            total = sb("total", [S, 4, HB], F32, one)
            inv = sb("inv", [S, 4, HB], F32, one)
        resid = sb("resid", [S, B, KT, P])
        with ExitStack() as three:
            cf_raw = [sb(f"cf_raw{i}", [P, KT // 2, LKP], F32, three) for i in range(2)]
            cf_hi = sb("cf_hi", [P, KT, LKP], F32R, three)
            cf_lo = sb("cf_lo", [P, KT, LKP], F32R, three)
            ct = [sb(f"ctx_tok{i}", [CR, CC, D], F32, three) for i in range(2)]
            x1 = sb("x1", [S, KT, P], F32, three)
            x2 = sb("x2", [S, KT, P], F32, three)
            x1_hi = sb("x1_hi", [P, KT, S], F32R, three)
            x1_lo = sb("x1_lo", [P, KT, S], F32R, three)
            cprob = sb("cprob", [S, LKP], F32, three)
            cprob_t = sb("cprob_t", [CR, CC, S], F32, three)
            ctop = sb("ctop", [S, 4], F32, three)
            stats2 = sb("stats2", [S, 2, 6], F32, three)
            mv2 = sb("mv2", [S, 4], F32, three)
        with ExitStack() as four:
            t_raw = sb("t_raw", [RA, B, S], F32, four)
            t_cat = sb("t_cat", [P, B, S], F32R, four)

        bank = [st.enter_context(nc.psum_tensor(f"bank{i}", [P, 512], F32)) for i in range(8)]
        PROD = bank[0:2]
        TURN = bank[2:4]
        SCORE = bank[4:6]
        HEADS = bank[6]
        TURN2 = [bank[5], bank[7]]

        const_in = sem("const_in")
        x_in = [sem(f"x_in{k}") for k in range(KT)]
        x_rounded, x_rest = sem("x_rounded"), sem("x_rest")
        w_in = [sem(f"w_in{i}") for i in range(3)]
        w0_mixed = [sem(f"w0_mixed{i}") for i in range(2)]
        w0_rounded = [sem(f"w0_rounded{i}") for i in range(3)]
        w0_rest = [sem(f"w0_rest{i}") for i in range(3)]
        w_mixed, w_rounded, w_rest = sem("w_mixed"), sem("w_rounded"), sem("w_rest")
        proj_done = sem("proj_done")
        qk_kept, v_kept = sem("qk_kept"), sem("v_kept")
        v_turned, v_tok_kept = sem("v_turned"), sem("v_tok_kept")
        scored, masked, topped, shifted = sem("scored"), sem("masked"), sem("topped"), sem("shifted")
        exped, inverted, normed = sem("exped"), sem("inverted"), sem("normed")
        prob_turned, prob_t_kept = sem("prob_turned"), sem("prob_t_kept")
        heads_done, heads_rounded = sem("heads_done"), sem("heads_rounded")
        heads_rest = sem("heads_rest")
        lin_in = [sem(f"lin_in{i}") for i in range(2)]
        lin_rounded, lin_rest, lin_done = sem("lin_rounded"), sem("lin_rest"), sem("lin_done")
        y_kept, y_turned, y_added = sem("y_kept"), sem("y_turned"), sem("y_added")
        y_stats = sem("y_stats")
        resid_in = sem("resid_in")
        power_set = sem("power_set")
        norm_aggr, norm_var, norm_rstd = sem("norm_aggr"), sem("norm_var"), sem("norm_rstd")
        x1_ready, x1_kept, x1_turned = sem("x1_ready"), sem("x1_kept"), sem("x1_turned")
        x1_rounded, x1_rest = sem("x1_rounded"), sem("x1_rest")
        cf_in = [sem(f"cf_in{i}") for i in range(2)]
        ct_in = [sem(f"ct_in{i}") for i in range(2)]
        cf_rounded, cf_rest = sem("cf_rounded"), sem("cf_rest")
        cscored, ctopped, cshifted = sem("cscored"), sem("ctopped"), sem("cshifted")
        cexped, cinverted, cnormed = sem("cexped"), sem("cinverted"), sem("cnormed")
        cturned, cprob_t_kept, cmixed = sem("cturned"), sem("cprob_t_kept"), sem("cmixed")
        cadded, cstats, caggr, cvar, crstd = (sem("cadded"), sem("cstats"), sem("caggr"),
                                              sem("cvar"), sem("crstd"))
        x2_ready, x2_kept, x2_turned = sem("x2_ready"), sem("x2_kept"), sem("x2_turned")
        x2_rounded, x2_rest = sem("x2_rounded"), sem("x2_rest")
        routed, t_filled, t_done = sem("routed"), sem("t_filled"), sem("t_done")
        t_masked, t_rounded, t_rest = sem("t_masked"), sem("t_rounded"), sem("t_rest")
        centred, out_ready, out_stored = sem("centred"), sem("out_ready"), sem("out_stored")
        out_ready2 = sem("out_ready2")

        block = st.enter_context(nc.Block())

        BEGIN = [(0, 0), (1, 0), (0, 1), (1, 1)]
        END = [(KT - 2, 0), (KT - 1, 0), (KT - 2, 1), (KT - 1, 1)]
        NP = 2 * KT

        @block.sync
        def _(sp):
            sp.dma_start(w_raw[0][:, 0:KT, :], qkv_w[0, 0]).then_inc(w_in[0], 16)
            sp.dma_start(x_raw[:, 0, :], x_feat[:, 0, :]).then_inc(x_in[0], 16)
            sp.dma_start(w_raw[1][:, 0:KT, :], qkv_w[0, 1]).then_inc(w_in[1], 16)
            for k in range(1, KT):
                sp.dma_start(x_raw[:, k, :], x_feat[:, k, :]).then_inc(x_in[k], 16)
            sp.dma_start(w_raw[2][:, :, :], qkv_w[0, 2]).then_inc(w_in[2], 16)

            for w in range(2):
                sp.wait_ge(w0_mixed[w], 1)
                sp.dma_start(w_raw[w][:, 0:KT, :], qkv_w[1, w]).then_inc(w_in[w], 16)
            sp.wait_ge(w0_rest[2], 1)
            sp.dma_start(w_raw[2][:, :, :], qkv_w[1, 2]).then_inc(w_in[2], 16)
            with sp.Fori(2, PAIRS) as s:
                for w in range(2):
                    sp.wait_ge(w_mixed, 2 * (s - 2) + w + 1)
                    sp.dma_start(w_raw[w][:, 0:KT, :], qkv_w[s, w]).then_inc(w_in[w], 16)
                sp.wait_ge(w_rest, 3 * (s - 2) + 3)
                sp.dma_start(w_raw[2][:, :, :], qkv_w[s, 2]).then_inc(w_in[2], 16)

            for u in range(2):
                sp.wait_ge(w_mixed, 2 * (PAIRS - 2) + u + 1)
                sp.dma_start(w_raw[u][:, 0:KT, :], wo_w[u]).then_inc(lin_in[u], 16)
            sp.wait_ge(proj_done, 6 * PAIRS)
            sp.dma_start(resid[:, :, :, :], x_tok).then_inc(resid_in, 16)

            def load_linear(t, u, weights, tile, kt):
                sp.wait_ge(lin_rest, t - 1)
                sp.dma_start(w_raw[u][:, 0:kt, :], weights[tile]).then_inc(lin_in[u], 16)

            for u in range(2):
                load_linear(2 + u, u, wo_w, 2 + u, KT)
            sp.wait_ge(heads_rest, 2 * PAIRS)
            for c in range(2):
                sp.dma_start(cf_raw[c][:, :, :], ctx_feat[0, c]).then_inc(cf_in[c], 16)
            sp.dma_start(ct[0][:, :, :], ctx_tok[0]).then_inc(ct_in[0], 16)
            for m, u in pairs_of_steps(sp, 2, KT // 2):
                load_linear(2 * m + u, u, wo_w, 2 * m + u, KT)
            for u in range(2):
                load_linear(KT + u, u, ffn_w, u, KT + 1)
            with sp.Fori(1, B) as b:
                for c in range(2):
                    sp.wait_ge(cf_rest, 2 * (b - 1) + c + 1)
                    sp.dma_start(cf_raw[c][:, :, :], ctx_feat[b, c]).then_inc(cf_in[c], 16)
            for m, u in pairs_of_steps(sp, 5, 8):
                load_linear(2 * m + u, u, ffn_w, 2 * m + u - 8, KT + 1)
            load_linear(16, 0, ffn_w, 8, KT + 1)
            for b in range(HB):
                sp.wait_ge(out_ready, b + 1)
                sp.dma_start(out[b], resid[:, b, :, :]).then_inc(out_stored, 16)
            for b in range(HB, B):
                if b % 2 == 0:
                    sp.wait_ge(out_ready, HB + (b - HB) // 2 + 1)
                else:
                    sp.wait_ge(out_ready2, (b - HB) // 2 + 1)
                sp.dma_start(out[b], resid[:, b, :, :]).then_inc(out_stored, 16)
            sp.wait_ge(out_stored, 16 * B)

        @block.tensor
        def _(pe):
            def project_part(k, w, h, to):
                for a, b in ((w_hi[w], x_hi), (w_hi[w], x_lo), (w_lo[w], x_hi)):
                    last = pe.matmul(to[:, 0:HT], a[:, k, :], b[:, k, HT * h:HT * h + HT],
                                     start=(k == 0 and b is x_hi and a is w_hi[w]),
                                     stop=(k == KT - 1 and a is w_lo[w]))
                return last

            def project(w, h, to):
                for k in range(KT):
                    last = project_part(k, w, h, to)
                last.then_inc(proj_done, 1)

            def turn_v(s, h):
                pe.wait_ge(v_kept, 2 * s + h + 1)
                for b in range(HB):
                    last = pe.transpose(TURN[h][0:S, b * P:(b + 1) * P],
                                        v_feat[:, HB * h + b, :], ident[:, :])
                last.then_inc(v_turned, 1)

            def score(p, u, r):
                for b in range(HB):
                    for h in range(2):
                        rows = slice(HD * h, HD * h + HD)
                        last = pe.matmul(SCORE[h][0:S, b * S:(b + 1) * S],
                                         qk[u][0][rows, HB * r + b, :],
                                         qk[u][1][rows, HB * r + b, :], start=True, stop=True)
                        if b == HB - 1:
                            last.then_inc(scored, 1)

            def turn_prob(p, r):
                for h in range(2):
                    a = 2 * r + h
                    pe.wait_ge(normed, 4 * p + a + 1)
                    if r == 0 and (h == 0 or isinstance(p, int) and p == PAIRS - 1):
                        pe.wait_ge(v_tok_kept, 2 * p + 1)
                    elif r == 0:
                        pe.wait_ge(v_tok_kept, 2 * p + 2)
                    else:
                        pe.wait_ge(prob_t_kept, 4 * p + h + 1)
                        if h == 1:
                            pe.wait_ge(v_tok_kept, 2 * p + 2)
                    for b in range(HB):
                        last = pe.transpose(TURN[h][0:S, b * S:(b + 1) * S],
                                            prob[a][:, b, :], ident[0:S, 0:S])
                    last.then_inc(prob_turned, 1)

            def mix_heads(p, r):
                pe.wait_ge(prob_t_kept, 4 * p + 2 * r + 2)
                pe.wait_ge(v_tok_kept, 2 * p + r + 1)
                if any_yet(2 * p + r):
                    pe.wait_ge(heads_rest, 2 * p + r)
                for b in range(HB):
                    for h in range(2):
                        last = pe.matmul(HEADS[HD * h:HD * h + HD, b * S:(b + 1) * S],
                                         v_tok[:, HB * r + b, HD * h:HD * h + HD],
                                         prob_t[2 * r + h][:, b, :], start=True, stop=True)
                last.then_inc(heads_done, 1)

            def step(s, u):
                p, up = s - 1, 1 - u
                pe.wait_ge(w_rest, 3 * (s - 1) + 1)
                pe.wait_ge(v_kept, 2 * (s - 1) + 1)
                project(0, 0, PROD[0])
                if any_yet(4 * (p - 1) + 4):
                    pe.wait_ge(prob_t_kept, 4 * (p - 1) + 4)
                turn_v(p, 1)
                pe.wait_ge(qk_kept, 4 * p + 4)
                if any_yet(4 * p):
                    pe.wait_ge(masked, 4 * p)
                score(p, up, 0)
                pe.wait_ge(v_kept, 2 * (s - 1) + 2)
                project(0, 1, PROD[1])
                pe.wait_ge(masked, 4 * p + 2)
                score(p, up, 1)
                pe.wait_ge(w_rest, 3 * (s - 1) + 2)
                pe.wait_ge(qk_kept, 4 * s + 1)
                project(1, 0, PROD[0])
                turn_prob(p, 0)
                pe.wait_ge(qk_kept, 4 * s + 2)
                project(1, 1, PROD[1])
                mix_heads(p, 0)
                turn_prob(p, 1)
                pe.wait_ge(w_rest, 3 * (s - 1) + 3)
                pe.wait_ge(qk_kept, 4 * s + 3)
                project(2, 0, PROD[0])
                mix_heads(p, 1)
                pe.wait_ge(qk_kept, 4 * s + 4)
                project(2, 1, PROD[1])
                pe.wait_ge(prob_t_kept, 4 * p + 3)
                turn_v(s, 0)

            for k, w in ([(k, 0) for k in range(4)] + [(k, 1) for k in range(4)]
                         + [(k, w) for k in range(4, KT) for w in range(2)]):
                if k == 0:
                    pe.wait_ge(w0_rest[w], 1)
                pe.wait_ge(x_rest, k + 1)
                for h in range(2):
                    last = project_part(k, w, h, (PROD, SCORE)[w][h])
                    if k == KT - 1:
                        last.then_inc(proj_done, 1)
            pe.wait_ge(w0_rest[2], 1)
            for h in range(2):
                pe.wait_ge(qk_kept, h + 1)
                project(2, h, PROD[h])
            pe.wait_ge(const_in, 16 * 5)
            turn_v(0, 0)
            step(1, 1)
            for m, u in pairs_of_steps(pe, 1, PAIRS // 2 - 1):
                step(2 * m + u, u)
            step(PAIRS - 2, 0)

            s, p = PAIRS - 1, PAIRS - 2
            pe.wait_ge(w_rest, 3 * (s - 1) + 1)
            pe.wait_ge(v_kept, 2 * (s - 1) + 1)
            project(0, 0, PROD[0])
            pe.wait_ge(prob_t_kept, 4 * (p - 1) + 4)
            turn_v(p, 1)
            pe.wait_ge(qk_kept, 4 * p + 4)
            pe.wait_ge(masked, 4 * p)
            score(p, 0, 0)
            pe.wait_ge(w_rest, 3 * (s - 1) + 2)
            pe.wait_ge(v_kept, 2 * (s - 1) + 2)
            project(1, 0, PROD[1])
            pe.wait_ge(masked, 4 * p + 2)
            score(p, 0, 1)
            pe.wait_ge(w_rest, 3 * (s - 1) + 3)
            pe.wait_ge(qk_kept, 4 * s + 1)
            project(2, 0, PROD[0])
            turn_prob(p, 0)
            pe.wait_ge(qk_kept, 4 * s + 2)
            pe.wait_ge(masked, 4 * p + 4)
            score(s, 1, 0)
            project(0, 1, PROD[1])
            mix_heads(p, 0)
            turn_prob(p, 1)
            pe.wait_ge(v_kept, 2 * s + 1)
            project(1, 1, PROD[0])
            mix_heads(p, 1)
            pe.wait_ge(prob_t_kept, 4 * p + 3)
            turn_v(s, 0)
            turn_prob(s, 0)
            pe.wait_ge(qk_kept, 4 * s + 3)
            project(2, 1, PROD[1])
            pe.wait_ge(qk_kept, 4 * s + 4)
            pe.wait_ge(masked, 4 * s + 2)
            score(s, 1, 1)
            mix_heads(s, 0)
            pe.wait_ge(prob_t_kept, 4 * s + 2)
            turn_v(s, 1)

            def part(k, u, h, to, first, last_k):
                for w, x in ((w_hi[u], act_hi), (w_hi[u], act_lo), (w_lo[u], act_hi)):
                    last = pe.matmul(to[:, 0:HT], w[:, k, :], x[:, k, HT * h:HT * h + HT],
                                     start=(k == first and w is w_hi[u] and x is act_hi),
                                     stop=(k == last_k and w is w_lo[u]))
                return last

            def turn_y(n, i):
                pe.wait_ge(y_kept, n + 1)
                if any_yet(n - 1):
                    pe.wait_ge(y_added, n - 1)
                for b in range(HB):
                    last = pe.transpose(TURN[i][0:S, b * P:(b + 1) * P],
                                        y_feat[:, i, b * S:(b + 1) * S], ident[:, :])
                last.then_inc(y_turned, 1)

            def product(n, i, u, h, extra=False, turn=True):
                if any_yet(n - 1):
                    pe.wait_ge(y_kept, n - 1)
                for k in range(KT):
                    if k == 2 and turn:
                        turn_y(n - 1, 1 - i)
                    last = part(k, u, h, PROD[i], 0, None if extra else KT - 1)
                if extra:
                    low_rank(i, u, h)
                else:
                    last.then_inc(lin_done, 1)

            def low_rank(i, u, h):
                rows = slice(HB * h, HB * h + HB)
                pe.matmul(PROD[i][:, 0:HT], w_hi[u][:, KT, :], t_cat[:, rows, :],
                          start=False, stop=False)
                pe.matmul(PROD[i][:, 0:HT], w_lo[u][0:EXTRA, KT, :], t_cat[0:EXTRA, rows, :],
                          start=False, stop=True).then_inc(lin_done, 1)

            for n, (j, h) in enumerate(BEGIN):
                if h == 0:
                    pe.wait_ge(lin_rest, j + 1)
                if n == 0:
                    pe.wait_ge(qk_kept, 4 * PAIRS)
                    pe.wait_ge(heads_rest, 2 * PAIRS - 2)
                    for k in range(KT - 1):
                        part(k, j, h, PROD[0], 0, None)
                    pe.wait_ge(heads_rest, 2 * PAIRS - 1)
                    part(KT - 1, j, h, PROD[0], 0, KT - 1).then_inc(lin_done, 1)
                    turn_prob(s, 1)
                elif n == 1:
                    pe.wait_ge(v_kept, 2 * PAIRS)
                    for k in range(KT):
                        last = part(k, j, h, PROD[1], 0, KT - 1)
                    last.then_inc(lin_done, 1)
                    mix_heads(s, 1)
                    pe.wait_ge(prob_t_kept, 4 * PAIRS)
                    turn_y(0, 0)
                elif n == 2:
                    pe.wait_ge(y_kept, 1)
                    for k in range(KT - 1):
                        if k == 2:
                            turn_y(1, 1)
                        part(k, j, h, PROD[0], 0, None)
                    pe.wait_ge(heads_rest, 2 * PAIRS)
                    part(KT - 1, j, h, PROD[0], 0, KT - 1).then_inc(lin_done, 1)
                else:
                    product(n, 1, j, h)
            for m, u in pairs_of_steps(pe, 1, KT // 2 - 1):
                pe.wait_ge(lin_rest, 2 * m + u + 1)
                for h in range(2):
                    product(2 * (2 * m + u) + h, h, u, h)
            for n, (j, h) in enumerate(END, NP - 4):
                if h == 0:
                    pe.wait_ge(lin_rest, j + 1)
                if n < NP - 1:
                    product(n, n % 2, j % 2, h)

            def turn_x1(b, to):
                pe.wait_ge(x1_ready, b + 1)
                for c in range(2):
                    for k in range(4):
                        last = pe.transpose(to[c][:, k * S:(k + 1) * S], x1[:, 4 * c + k, :],
                                            ident[0:S, 0:S])
                    last.then_inc(x1_turned, 1)

            pe.wait_ge(y_kept, NP - 2)
            for k in range(KT):
                if k == 2:
                    turn_y(NP - 2, 0)
                if k == 6:
                    turn_x1(0, TURN2)
                last = part(k, 1, 1, PROD[1], 0, KT - 1)
            last.then_inc(lin_done, 1)

            def cross_score(b):
                pe.wait_ge(x1_rest, 2 * b + 2)
                if any_yet(b):
                    pe.wait_ge(cexped, b)
                for c in range(2):
                    pe.wait_ge(cf_rest, 2 * b + c + 1)
                    for k in range(4 * c, 4 * c + 4):
                        for w, x in ((x1_hi, cf_hi), (x1_hi, cf_lo), (x1_lo, cf_hi)):
                            last = pe.matmul(SCORE[0][0:S, 0:LKP], w[:, k, :], x[:, k, :],
                                             start=(k == 0 and w is x1_hi and x is cf_hi),
                                             stop=(k == KT - 1 and w is x1_lo))
                    last.then_inc(cscored, 1)

            def turn_x2(b):
                pe.wait_ge(x2_ready, b + 1)
                if any_yet(2 * b):
                    pe.wait_ge(x2_rest, 2 * b)
                for c in range(2):
                    for k in range(4):
                        last = pe.transpose(TURN2[c][:, k * S:(k + 1) * S], x2[:, 4 * c + k, :],
                                            ident[0:S, 0:S])
                    last.then_inc(x2_turned, 1)

            def cross_mix(b, u, m):
                pe.wait_ge(cprob_t_kept, b + 1)
                pe.wait_ge(ct_in[u], 16 * m + 16)
                if any_yet(2 * b):
                    pe.wait_ge(cadded, 2 * b)
                for n in range(2):
                    for c in range(CC):
                        last = pe.matmul(PROD[n][0:S, :], cprob_t[:, c, :],
                                         ct[u][:, c, 512 * n:512 * n + 512],
                                         start=(c == 0), stop=(c == CC - 1))
                    last.then_inc(cmixed, 1)

            def turn_cprob(b):
                pe.wait_ge(cnormed, b + 1)
                if any_yet(b):
                    pe.wait_ge(cprob_t_kept, b)
                for c in range(CC):
                    last = pe.transpose(HEADS[0:CR, c * S:(c + 1) * S],
                                        cprob[:, c * CR:(c + 1) * CR], ident[0:S, 0:S])
                last.then_inc(cturned, 1)

            def cross_step(b, u, m):
                known = isinstance(b, int)
                cross_score(b)
                if not known or b + 1 < B:
                    pe.wait_ge(x1_rest, 2 * b + 2)
                    turn_x1(b + 1, TURN)
                cross_mix(b - 1, 1 - u, m - 1 if u == 0 else m)
                if not known or b >= 2:
                    turn_x2(b - 2)
                turn_cprob(b)

            cross_score(0)
            turn_y(NP - 1, 1)
            pe.wait_ge(y_added, NP)
            pe.wait_ge(y_kept, NP)
            turn_x1(1, TURN)
            turn_cprob(0)
            cross_step(1, 1, 0)
            for m, u in pairs_of_steps(pe, 1, 3):
                cross_step(2 * m + u, u, m)
            cross_step(6, 0, 3)
            cross_step(7, 1, 3)
            cross_mix(7, 1, 3)
            turn_x2(6)

            def lora(h):
                for k in range(KT):
                    last = part(k, 0, h, TURN[h], 0, KT - 1)
                last.then_inc(t_done, 1)

            pe.wait_ge(lin_rest, KT + 1)
            lora(0)
            pe.wait_ge(lin_rest, KT + 2)
            pe.wait_ge(cadded, 2 * B)
            for k in range(KT):
                if k == 4:
                    turn_x2(7)
                part(k, 1, 0, PROD[0], 0, None)
            pe.wait_ge(t_rest, 1)
            low_rank(0, 1, 0)
            pe.wait_ge(x2_rest, 2 * B)
            lora(1)
            for k in range(KT):
                if k == 2:
                    turn_y(NP, 0)
                part(k, 1, 1, PROD[1], 0, None)
            pe.wait_ge(t_rest, 2)
            low_rank(1, 1, 1)
            for m, u in pairs_of_steps(pe, 5, 7):
                pe.wait_ge(lin_rest, 2 * m + u + 1)
                for h in range(2):
                    product(NP + 2 * (2 * m + u - 9) + h, h, u, h, extra=True)
            pe.wait_ge(lin_rest, 15)
            for h in range(2):
                product(NP + 10 + h, h, 0, h, extra=True)
            for n, (j, h) in enumerate(END, 2 * NP - 4):
                if h == 0:
                    pe.wait_ge(lin_rest, j + 10)
                product(n, n % 2, (j + 1) % 2, h, extra=True)
            turn_y(2 * NP - 1, 1)

        @block.scalar
        def _(act):
            act.dma_start(turn[:, :], rotary).then_inc(const_in, 16)
            act.dma_start(ident[:, :], identity).then_inc(const_in, 16)
            act.dma_start(mask[:, :], causal).then_inc(const_in, 16)
            act.dma_start(route_c[:, :], route).then_inc(const_in, 16)
            act.dma_start(starts_i[:, :], starts).then_inc(const_in, 16)

            def round_w(s, w):
                if w < 2:
                    act.wait_ge(w_mixed, 2 * (s - 1) + w + 1)
                else:
                    act.wait_ge(w_in[2], 16 * s + 16)
                act.wait_ge(proj_done, 6 * (s - 1) + 2 * w + 2)
                src = w_mix if w < 2 else w_raw[2]
                act.activation(w_hi[w][:, 0:KT, :], src[:, :, :], ACT.Copy).then_inc(w_rounded, 1)

            def keep_v(s, h, done, frm):
                act.wait_ge(proj_done, done)
                if any_yet(2 * (s - 1) + h + 1):
                    act.wait_ge(v_turned, 2 * (s - 1) + h + 1)
                act.activation(v_feat[:, HB * h:HB * h + HB, :], frm[:, 0:HT],
                               ACT.Copy).then_inc(v_kept, 1)

            def keep_v_tok(s, h):
                act.wait_ge(v_turned, 2 * s + h + 1)
                act.activation(v_tok[:, HB * h:HB * h + HB, :], TURN[h][0:S, :],
                               ACT.Copy).then_inc(v_tok_kept, 1)

            def exponentials(p, r):
                for h in range(2):
                    a = 2 * r + h
                    act.wait_ge(shifted, 4 * p + a + 1)
                    for b in range(HB):
                        last = act.activation(prob[a][:, b, :], prob[a][:, b, :], ACT.Exp,
                                              bias=shift[:, a, b:b + 1], scale=SCORE_SCALE,
                                              accum_out=total[:, a, b:b + 1])
                    last.then_inc(exped, 1)

            def keep_prob_t(p, r):
                for h in range(2):
                    a = 2 * r + h
                    act.wait_ge(prob_turned, 4 * p + a + 1)
                    if any_yet(2 * (p - 1) + r + 1):
                        act.wait_ge(heads_done, 2 * (p - 1) + r + 1)
                    act.activation(prob_t[a][:, :, :], TURN[h][0:S, 0:HT],
                                   ACT.Copy).then_inc(prob_t_kept, 1)

            def round_heads(p, r):
                act.wait_ge(heads_done, 2 * p + r + 1)
                act.activation(act_hi[:, p, HT * r:HT * r + HT], HEADS[:, 0:HT],
                               ACT.Copy).then_inc(heads_rounded, 1)

            def step(s):
                p = s - 1
                round_w(s, 2)
                keep_v_tok(p, 1)
                exponentials(p, 0)
                round_w(s + 1, 0)
                exponentials(p, 1)
                keep_prob_t(p, 0)
                round_w(s + 1, 1)
                round_heads(p, 0)
                keep_prob_t(p, 1)
                keep_v(s, 0, 6 * s + 5, PROD[0])
                round_heads(p, 1)
                keep_v(s, 1, 6 * s + 6, PROD[1])
                keep_v_tok(s, 0)

            def round_x(k):
                act.wait_ge(x_in[k], 16)
                act.activation(x_hi[:, k, :], x_raw[:, k, :], ACT.Copy).then_inc(x_rounded, 1)

            act.wait_ge(w0_mixed[0], 1)
            act.activation(w_hi[0][:, 0:KT, :], w_mix0[:, :, :], ACT.Copy).then_inc(w0_rounded[0], 1)
            round_x(0)
            round_x(1)
            act.wait_ge(w0_mixed[1], 1)
            act.activation(w_hi[1][:, 0:KT, :], w_mix[:, :, :], ACT.Copy).then_inc(w0_rounded[1], 1)
            for k in range(2, KT):
                round_x(k)
            act.wait_ge(w_in[2], 16)
            act.activation(w_hi[2][:, :, :], w_raw[2][:, :, :], ACT.Copy).then_inc(w0_rounded[2], 1)
            round_w(1, 0)
            round_w(1, 1)
            keep_v(0, 0, 5, PROD[0])
            keep_v(0, 1, 6, PROD[1])
            keep_v_tok(0, 0)
            step(1)
            for m, u in pairs_of_steps(act, 1, PAIRS // 2 - 1):
                step(2 * m + u)
            step(PAIRS - 2)

            def round_linear(t, u, kt, arrived):
                act.wait_ge(lin_in[u], 16 * arrived)
                act.activation(w_hi[u][:, 0:kt, :], w_raw[u][:, 0:kt, :],
                               ACT.Copy).then_inc(lin_rounded, 1)

            def keep_y(n, i):
                act.wait_ge(lin_done, n + 1)
                if any_yet(n - 1):
                    act.wait_ge(y_turned, n - 1)
                act.activation(y_feat[:, i, :], PROD[i][:, 0:HT], ACT.Copy).then_inc(y_kept, 1)

            s, p = PAIRS - 1, PAIRS - 2
            round_w(s, 2)
            keep_v_tok(p, 1)
            exponentials(p, 0)
            exponentials(p, 1)
            keep_v(s, 0, 6 * s + 3, PROD[0])
            keep_prob_t(p, 0)
            exponentials(s, 0)
            act.wait_ge(proj_done, 6 * s + 4)
            round_linear(0, 0, KT, 1)
            round_heads(p, 0)
            keep_prob_t(p, 1)
            act.wait_ge(proj_done, 6 * s + 5)
            round_linear(1, 1, KT, 1)
            round_heads(p, 1)
            keep_v_tok(s, 0)
            keep_prob_t(s, 0)
            keep_v(s, 1, 6 * s + 6, PROD[1])
            round_heads(s, 0)
            keep_v_tok(s, 1)
            exponentials(s, 1)
            keep_prob_t(s, 1)
            keep_y(0, 0)
            round_heads(s, 1)
            keep_y(1, 1)
            keep_y(2, 0)
            round_linear(2, 0, KT, 2)
            keep_y(3, 1)
            round_linear(3, 1, KT, 2)

            def round_cf(b, c):
                act.wait_ge(cf_in[c], 16 * b + 16)
                if any_yet(2 * (b - 1) + c + 1):
                    act.wait_ge(cscored, 2 * (b - 1) + c + 1)
                act.activation(cf_hi[:, 4 * c:4 * c + 4, :], cf_raw[c][:, :, :],
                               ACT.Copy).then_inc(cf_rounded, 1)

            round_cf(0, 0)
            round_cf(0, 1)
            for m, u in pairs_of_steps(act, 1, KT // 2 - 1):
                keep_y(2 * (2 * m + u), 0)
                keep_y(2 * (2 * m + u) + 1, 1)
                round_linear(2 * m + u + 2, u, KT, m + 2)

            def keep_x1(b):
                act.wait_ge(x1_ready, b + 1)
                act.activation(resid[:, b, :, :], x1[:, :, :], ACT.Copy).then_inc(x1_kept, 1)

            def round_x1(b, frm):
                for c in range(2):
                    act.wait_ge(x1_turned, 2 * b + c + 1)
                    if any_yet(2 * b):
                        act.wait_ge(cscored, 2 * b)
                    act.activation(x1_hi[:, 4 * c:4 * c + 4, :], frm[c][:, 0:4 * S],
                                   ACT.Copy).then_inc(x1_rounded, 1)

            def round_x2(b):
                for c in range(2):
                    act.wait_ge(x2_turned, 2 * b + c + 1)
                    to = act_hi[:, :, :].rearrange("p k (b s) -> p k b s", b=B)
                    act.activation(to[:, 4 * c:4 * c + 4, b, :], TURN2[c][:, 0:4 * S],
                                   ACT.Copy).then_inc(x2_rounded, 1)

            def keep_x2(b):
                act.wait_ge(x2_ready, b + 1)
                act.activation(resid[:, b, :, :], x2[:, :, :], ACT.Copy).then_inc(x2_kept, 1)

            def cross_step(b, u):
                known = isinstance(b, int)
                if not known or b + 1 < B:
                    round_cf(b + 1, 0)
                act.wait_ge(cshifted, b + 1)
                act.activation(cprob[:, 0:LK], SCORE[0][0:S, 0:LK], ACT.Exp,
                               bias=ctop[:, 1:2], accum_out=ctop[:, 2:3]).then_inc(cexped, 1)
                if not known or b + 1 < B:
                    if known and b == 0:
                        keep_y(NP - 1, 1)
                    round_x1(b + 1, TURN)
                    round_cf(b + 1, 1)
                if not known or b >= 2:
                    keep_x2(b - 2)
                if not known or b + 2 < B:
                    keep_x1(b + 2)
                if not known or b >= 2:
                    round_x2(b - 2)
                act.wait_ge(cturned, b + 1)
                if any_yet(b):
                    act.wait_ge(cmixed, 2 * b)
                act.activation(cprob_t[:, :, :], HEADS[0:CR, 0:CC * S],
                               ACT.Copy).then_inc(cprob_t_kept, 1)
                if not known or b + 1 < B:
                    act.dma_start(ct[1 - u][:, :, :], ctx_tok[b + 1]).then_inc(ct_in[1 - u], 16)

            for n in range(NP - 4, NP - 1):
                keep_y(n, n % 2)
            keep_x1(0)
            round_x1(0, TURN2)
            keep_x1(1)
            cross_step(0, 0)
            cross_step(1, 1)
            for m, u in pairs_of_steps(act, 1, 3):
                cross_step(2 * m + u, u)
            cross_step(6, 0)
            round_linear(KT, 0, KT + 1, 5)
            round_linear(KT + 1, 1, KT + 1, 5)
            cross_step(7, 1)
            keep_x2(6)
            round_x2(6)

            def round_t(h):
                rows = slice(HB * h, HB * h + HB)
                act.wait_ge(t_masked, h + 1)
                act.wait_ge(t_filled, 2)
                act.activation(t_cat[0:RA, rows, :], t_raw[:, rows, :],
                               ACT.Copy).then_inc(t_rounded, 1)

            round_t(0)
            keep_x2(7)
            round_x2(7)
            keep_y(NP, 0)
            round_t(1)
            round_linear(10, 0, KT + 1, 6)
            keep_y(NP + 1, 1)
            round_linear(11, 1, KT + 1, 6)
            for m, u in pairs_of_steps(act, 5, 7):
                keep_y(NP + 2 * (2 * m + u - 9), 0)
                keep_y(NP + 2 * (2 * m + u - 9) + 1, 1)
                round_linear(2 * m + u + 2, u, KT + 1, m + 2)
            keep_y(2 * NP - 6, 0)
            keep_y(2 * NP - 5, 1)
            round_linear(16, 0, KT + 1, 9)
            for n in range(2 * NP - 4, 2 * NP):
                keep_y(n, n % 2)
            act.wait_ge(centred, 1)
            for b in range(HB + 1, B, 2):
                act.activation(resid[:, b, :, :], resid[:, b, :, :], ACT.Identity,
                               bias=centre[:, b, :], scale=rstd[:, b, :]).then_inc(out_ready2, 1)

        @block.vector
        def _(dve):
            dve.wait_ge(w_in[0], 16)
            raw = w_raw[0][:, 0:KT, :].rearrange("p k (h t i) -> p (k h) t i", h=2, t=2)
            mix = w_mix0[:, :, :].rearrange("p k (h t i) -> p (k h) t i", h=2, t=2)
            dve.tensor_tensor(mix[:, :, 0, :], raw[:, :, 0, :], raw[:, :, 1, :], ALU.add)
            dve.tensor_tensor(mix[:, :, 1, :], raw[:, :, 0, :], raw[:, :, 1, :],
                              ALU.subtract).then_inc(w0_mixed[0], 1)
            dve.wait_ge(w0_rounded[0], 1)
            dve.tensor_tensor(w_lo[0][:, 0:KT, :], w_mix0[:, :, :],
                              w_hi[0][:, 0:KT, :].bitcast(F32), ALU.subtract).then_inc(w0_rest[0], 1)
            for k in range(KT):
                dve.wait_ge(x_rounded, k + 1)
                dve.tensor_tensor(x_lo[:, k, :], x_raw[:, k, :], x_hi[:, k, :].bitcast(F32),
                                  ALU.subtract).then_inc(x_rest, 1)
            dve.wait_ge(w0_rounded[2], 1)
            dve.tensor_tensor(w_lo[2][:, :, :], w_raw[2][:, :, :],
                              w_hi[2][:, :, :].bitcast(F32), ALU.subtract).then_inc(w0_rest[2], 1)

            dve.wait_ge(const_in, 16 * 5)
            dve.tensor_copy(starts_f[:, :], starts_i[:, :]).then_inc(routed, 1)
            dve.wait_ge(routed, 1)
            for i in range(NA + 1):
                dve.tensor_scalar(passed[:, i, :], route_c[:, 0:B], starts_f[:, i:i + 1], None,
                                  ALU.is_ge).then_inc(routed, 1)
            for i in range(1, NA + 1):
                dve.wait_ge(routed, 4 + i)
                dve.tensor_tensor(passed[:, 0, :], passed[:, 0, :], passed[:, i, :],
                                  ALU.add).then_inc(routed, 1)
            dve.wait_ge(routed, 5 + NA)
            dve.tensor_scalar(sel[:, :], passed[:, 0, :], route_c[:, B:B + 1], None,
                              ALU.is_equal).then_inc(routed, 1)

            scale = turn[:, :].unsqueeze(1).broadcast_to([P, HB, S])
            hidden = mask[:, :].unsqueeze(1).broadcast_to([S, HB, S])

            def keep_qk(u, w, h, done, frm):
                dve.wait_ge(proj_done, done)
                dve.tensor_tensor(qk[u][w][:, HB * h:HB * h + HB, :],
                                  frm[:, 0:HT].rearrange("p (b s) -> p b s", b=HB),
                                  scale, ALU.mult).then_inc(qk_kept, 1)

            def mask_and_top(p, r):
                for h in range(2):
                    a = 2 * r + h
                    dve.wait_ge(scored, 4 * p + a + 1)
                    if any_yet(4 * (p - 1) + a + 1):
                        dve.wait_ge(prob_turned, 4 * (p - 1) + a + 1)
                    dve.tensor_tensor(prob[a][:, :, :],
                                      SCORE[h][0:S, 0:HT].rearrange("p (b s) -> p b s", b=HB),
                                      hidden, ALU.add).then_inc(masked, 1)
                for h in range(2):
                    a = 2 * r + h
                    dve.wait_ge(masked, 4 * p + a + 1)
                    dve.tensor_reduce(top[:, a, :], prob[a][:, :, :], AX.X,
                                      ALU.max).then_inc(topped, 1)
                for h in range(2):
                    a = 2 * r + h
                    dve.wait_ge(topped, 4 * p + a + 1)
                    dve.tensor_scalar(shift[:, a, :], top[:, a, :], -SCORE_SCALE, None,
                                      ALU.mult).then_inc(shifted, 1)

            def normalise(p, r):
                for h in range(2):
                    a = 2 * r + h
                    dve.wait_ge(exped, 4 * p + a + 1)
                    dve.reciprocal(inv[:, a, :], total[:, a, :]).then_inc(inverted, 1)
                for h in range(2):
                    a = 2 * r + h
                    dve.wait_ge(inverted, 4 * p + a + 1)
                    dve.tensor_tensor(prob[a][:, :, :], prob[a][:, :, :],
                                      inv[:, a, :].unsqueeze(2).broadcast_to([S, HB, S]),
                                      ALU.mult).then_inc(normed, 1)

            def rest_heads(p, r):
                dve.wait_ge(heads_rounded, 2 * p + r + 1)
                dve.tensor_tensor(act_lo[:, p, HT * r:HT * r + HT], HEADS[:, 0:HT],
                                  act_hi[:, p, HT * r:HT * r + HT].bitcast(F32),
                                  ALU.subtract).then_inc(heads_rest, 1)

            def step(s, u):
                p = s - 1
                if any_yet(4 * (s - 1)):
                    dve.wait_ge(scored, 4 * (s - 1))
                keep_qk(u, 0, 0, 6 * s + 1, PROD[0])
                mask_and_top(p, 0)
                keep_qk(u, 0, 1, 6 * s + 2, PROD[1])
                normalise(p, 0)
                mask_and_top(p, 1)
                keep_qk(u, 1, 0, 6 * s + 3, PROD[0])
                normalise(p, 1)
                keep_qk(u, 1, 1, 6 * s + 4, PROD[1])
                rest_heads(p, 0)
                rest_heads(p, 1)

            for w in range(2):
                for h in range(2):
                    keep_qk(0, w, h, 2 * w + h + 1, (PROD, SCORE)[w][h])
            step(1, 1)
            for m, u in pairs_of_steps(dve, 1, PAIRS // 2 - 1):
                step(2 * m + u, u)
            step(PAIRS - 2, 0)

            s, p = PAIRS - 1, PAIRS - 2
            dve.wait_ge(scored, 4 * (s - 1))
            keep_qk(1, 0, 0, 6 * s + 1, PROD[0])
            mask_and_top(p, 0)
            keep_qk(1, 1, 0, 6 * s + 2, PROD[1])
            normalise(p, 0)
            mask_and_top(p, 1)
            normalise(p, 1)
            mask_and_top(s, 0)
            keep_qk(1, 0, 1, 6 * s + 4, PROD[1])
            normalise(s, 0)
            rest_heads(p, 0)
            keep_qk(1, 1, 1, 6 * s + 5, PROD[0])
            rest_heads(p, 1)
            mask_and_top(s, 1)
            rest_heads(s, 0)
            normalise(s, 1)
            rest_heads(s, 1)

            def add_y(n, i, j, h):
                rows = slice(HB * h, HB * h + HB)
                dve.wait_ge(y_turned, n + 1)
                dve.tensor_tensor(resid[:, rows, j, :],
                                  TURN[i][0:S, :].rearrange("p (b s) -> p b s", b=HB),
                                  resid[:, rows, j, :], ALU.add).then_inc(y_added, 1)
                dve.wait_ge(y_added, n + 1)
                for b in range(HB * h, HB * h + HB):
                    last = dve.bn_stats(stats[:, b, j, :], resid[:, b, j, :])
                last.then_inc(y_stats, 1)

            def row_norms(q, n, h):
                rows = slice(HB * h, HB * h + HB)
                dve.wait_ge(y_stats, n + 1)
                for b in range(HB * h, HB * h + HB):
                    last = dve.bn_aggr(mv[:, b, :], stats[:, b, :, :])
                last.then_inc(norm_aggr, 1)
                dve.wait_ge(norm_aggr, q + 1)
                dve.tensor_scalar(var_eps[:, rows], mv[:, rows, 1], EPS, None,
                                  ALU.add).then_inc(norm_var, 1)
                dve.wait_ge(norm_rstd, q + 1)

            dve.wait_ge(resid_in, 16)
            for n, (j, h) in enumerate(BEGIN):
                add_y(n, n % 2, j, h)
            for m, u in pairs_of_steps(dve, 1, KT // 2 - 1):
                for h in range(2):
                    add_y(2 * (2 * m + u) + h, h, 2 * m + u, h)

            def norm_x1(b):
                if any_yet(b):
                    dve.wait_ge(x1_turned, 2 * b)
                    dve.wait_ge(x1_kept, b)
                dve.tensor_scalar(x1[:, :, :], resid[:, b, :, :], mv[:, b, 0:1], rstd[:, b, :],
                                  ALU.subtract, ALU.mult).then_inc(x1_ready, 1)

            def rest_x1(b, frm):
                for c in range(2):
                    dve.wait_ge(x1_rounded, 2 * b + c + 1)
                    dve.tensor_tensor(x1_lo[:, 4 * c:4 * c + 4, :],
                                      frm[c][:, 0:4 * S].rearrange("p (k s) -> p k s", k=4),
                                      x1_hi[:, 4 * c:4 * c + 4, :].bitcast(F32),
                                      ALU.subtract).then_inc(x1_rest, 1)

            def rest_x2(b):
                lo = act_lo[:, :, :].rearrange("p k (b s) -> p k b s", b=B)
                hi = act_hi[:, :, :].bitcast(F32).rearrange("p k (b s) -> p k b s", b=B)
                for c in range(2):
                    ks = slice(4 * c, 4 * c + 4)
                    dve.wait_ge(x2_rounded, 2 * b + c + 1)
                    dve.tensor_tensor(lo[:, ks, b, :],
                                      TURN2[c][:, 0:4 * S].rearrange("p (k s) -> p k s", k=4),
                                      hi[:, ks, b, :], ALU.subtract).then_inc(x2_rest, 1)

            def sum_x2(b):
                if any_yet(b):
                    dve.wait_ge(x2_turned, 2 * b)
                    dve.wait_ge(x2_kept, b)
                dve.wait_ge(x1_kept, b + 1)
                for n in range(2):
                    ks = slice(4 * n, 4 * n + 4)
                    dve.wait_ge(cmixed, 2 * b + n + 1)
                    dve.tensor_tensor(x2[:, ks, :],
                                      PROD[n][0:S, :].rearrange("p (k s) -> p k s", k=4),
                                      resid[:, b, ks, :], ALU.add).then_inc(cadded, 1)
                for n in range(2):
                    dve.wait_ge(cadded, 2 * b + n + 1)
                    last = dve.bn_stats(stats2[:, n, :], x2[:, 4 * n:4 * n + 4, :])
                last.then_inc(cstats, 1)
                dve.wait_ge(const_in, 16 * 5)
                dve.wait_ge(cstats, b + 1)
                dve.bn_aggr(mv2[:, 0:2], stats2[:, :, :]).then_inc(caggr, 1)
                dve.wait_ge(caggr, b + 1)
                dve.tensor_scalar(mv2[:, 2:3], mv2[:, 1:2], EPS, None, ALU.add).then_inc(cvar, 1)

            def norm_x2(b):
                dve.wait_ge(crstd, b + 1)
                dve.tensor_scalar(x2[:, :, :], x2[:, :, :], mv2[:, 0:1], mv2[:, 3:4],
                                  ALU.subtract, ALU.mult).then_inc(x2_ready, 1)

            def cross_step(b):
                known = isinstance(b, int)
                if not known or b >= 2:
                    sum_x2(b - 2)
                dve.wait_ge(cscored, 2 * b + 2)
                if any_yet(b):
                    dve.wait_ge(cturned, b)
                dve.tensor_reduce(ctop[:, 0:1], SCORE[0][0:S, 0:LK], AX.X,
                                  ALU.max).then_inc(ctopped, 1)
                dve.wait_ge(ctopped, b + 1)
                dve.tensor_scalar(ctop[:, 1:2], ctop[:, 0:1], -1.0, None,
                                  ALU.mult).then_inc(cshifted, 1)
                if not known or b >= 2:
                    norm_x2(b - 2)
                if known and b == 0:
                    add_y(NP - 1, 1, KT - 1, 1)
                if not known or b + 1 < B:
                    rest_x1(b + 1, TURN)
                dve.wait_ge(cexped, b + 1)
                dve.reciprocal(ctop[:, 3:4], ctop[:, 2:3]).then_inc(cinverted, 1)
                dve.wait_ge(cinverted, b + 1)
                dve.tensor_scalar(cprob[:, 0:LK], cprob[:, 0:LK], ctop[:, 3:4], None,
                                  ALU.mult).then_inc(cnormed, 1)
                if known and b == 0:
                    row_norms(1, NP - 1, 1)
                if not known or b + 2 < B:
                    norm_x1(b + 2)
                if not known or b >= 2:
                    rest_x2(b - 2)

            add_y(NP - 4, 0, KT - 2, 0)
            add_y(NP - 3, 1, KT - 1, 0)
            row_norms(0, NP - 3, 0)
            norm_x1(0)
            add_y(NP - 2, 0, KT - 2, 1)
            rest_x1(0, TURN2)
            norm_x1(1)
            cross_step(0)
            cross_step(1)
            for m, u in pairs_of_steps(dve, 1, 3):
                cross_step(2 * m + u)
            cross_step(6)
            cross_step(7)

            def mask_t(h):
                rows = slice(HB * h, HB * h + HB)
                dve.wait_ge(t_done, h + 1)
                dve.tensor_tensor(t_raw[:, rows, :],
                                  TURN[h][0:RA, 0:HT].rearrange("p (b s) -> p b s", b=HB),
                                  sel[:, rows].unsqueeze(2).broadcast_to([RA, HB, S]),
                                  ALU.mult).then_inc(t_masked, 1)

            def rest_t(h):
                rows = slice(HB * h, HB * h + HB)
                dve.wait_ge(t_rounded, h + 1)
                dve.tensor_tensor(t_cat[EXTRA:EXTRA + RA, rows, :], t_raw[:, rows, :],
                                  t_cat[0:RA, rows, :].bitcast(F32),
                                  ALU.subtract).then_inc(t_rest, 1)

            dve.wait_ge(cf_rest, 2 * B)
            dve.memset(t_cat[32:EXTRA, :, :].bitcast(F32), 1.0).then_inc(t_filled, 1)
            dve.memset(t_cat[EXTRA:P, :, :].bitcast(F32), 0.0).then_inc(t_filled, 1)
            sum_x2(6)
            norm_x2(6)
            rest_x2(6)
            sum_x2(7)
            norm_x2(7)
            dve.wait_ge(t_filled, 2)
            mask_t(0)
            rest_t(0)
            rest_x2(7)
            mask_t(1)
            rest_t(1)
            for h in range(2):
                add_y(NP + h, h, 0, h)
            for m, u in pairs_of_steps(dve, 5, 7):
                for h in range(2):
                    add_y(NP + 2 * (2 * m + u - 9) + h, h, 2 * m + u - 9, h)
            for h in range(2):
                add_y(NP + 10 + h, h, 5, h)

            def norm_out(b):
                dve.tensor_scalar(resid[:, b, :, :], resid[:, b, :, :], mv[:, b, 0:1],
                                  rstd[:, b, :], ALU.subtract, ALU.mult).then_inc(out_ready, 1)

            add_y(2 * NP - 4, 0, KT - 2, 0)
            add_y(2 * NP - 3, 1, KT - 1, 0)
            row_norms(2, 2 * NP - 3, 0)
            for b in range(HB):
                norm_out(b)
            add_y(2 * NP - 2, 0, KT - 2, 1)
            add_y(2 * NP - 1, 1, KT - 1, 1)
            row_norms(3, 2 * NP - 1, 1)
            dve.scalar_tensor_tensor(out=centre[:, HB:B, :], in0=mv[:, HB:B, 0:1], scalar=-1.0,
                                     in1=rstd[:, HB:B, :], op0=ALU.mult,
                                     op1=ALU.mult).then_inc(centred, 1)
            for b in range(HB, B, 2):
                norm_out(b)

        @block.gpsimd
        def _(pool):
            pool.memset(minus_half[:, :], -0.5).then_inc(power_set, 1)

            def mix_w(w):
                raw = w_raw[w][:, 0:KT, :].rearrange("p k (h t i) -> p (k h) t i", h=2, t=2)
                mix = w_mix[:, :, :].rearrange("p k (h t i) -> p (k h) t i", h=2, t=2)
                pool.tensor_tensor(mix[:, :, 0, :], raw[:, :, 0, :], raw[:, :, 1, :], ALU.add)
                return pool.tensor_tensor(mix[:, :, 1, :], raw[:, :, 0, :], raw[:, :, 1, :],
                                          ALU.subtract)

            def rest_w(w):
                src = w_mix if w < 2 else w_raw[2]
                return pool.tensor_tensor(w_lo[w][:, 0:KT, :], src[:, :, :],
                                          w_hi[w][:, 0:KT, :].bitcast(F32), ALU.subtract)

            def prepare_w(s):
                for w in range(2):
                    pool.wait_ge(w_in[w], 16 * s + 16)
                    if any_yet(3 * (s - 2) + w + 2 if w == 0 else 3 * (s - 1) + 1):
                        pool.wait_ge(w_rest, 3 * (s - 2) + 2 if w == 0 else 3 * (s - 1) + 1)
                    mix_w(w).then_inc(w_mixed, 1)
                    pool.wait_ge(w_rounded, 3 * (s - 1) + w + 1)
                    rest_w(w).then_inc(w_rest, 1)
                pool.wait_ge(w_rounded, 3 * (s - 1) + 3)
                rest_w(2).then_inc(w_rest, 1)

            pool.wait_ge(w_in[1], 16)
            mix_w(1).then_inc(w0_mixed[1], 1)
            pool.wait_ge(w0_rounded[1], 1)
            rest_w(1).then_inc(w0_rest[1], 1)
            pool.wait_ge(w0_rest[1], 1)
            prepare_w(1)
            for m, u in pairs_of_steps(pool, 1, PAIRS // 2):
                prepare_w(2 * m + u)

            def rest_linear(t, u, kt):
                pool.wait_ge(lin_rounded, t + 1)
                pool.tensor_tensor(w_lo[u][:, 0:kt, :], w_raw[u][:, 0:kt, :],
                                   w_hi[u][:, 0:kt, :].bitcast(F32),
                                   ALU.subtract).then_inc(lin_rest, 1)

            def rest_cf(b):
                for c in range(2):
                    pool.wait_ge(cf_rounded, 2 * b + c + 1)
                    pool.tensor_tensor(cf_lo[:, 4 * c:4 * c + 4, :], cf_raw[c][:, :, :],
                                       cf_hi[:, 4 * c:4 * c + 4, :].bitcast(F32),
                                       ALU.subtract).then_inc(cf_rest, 1)

            def rows_power(q, h):
                rows = slice(HB * h, HB * h + HB)
                pool.wait_ge(norm_var, q + 1)
                pool.tensor_tensor(rstd[:, rows, 0], var_eps[:, rows], minus_half[:, :],
                                   ALU.pow).then_inc(norm_rstd, 1)

            def cross_power(b):
                pool.wait_ge(cvar, b + 1)
                pool.tensor_tensor(mv2[:, 3:4], mv2[:, 2:3], minus_half[:, 0:1],
                                   ALU.pow).then_inc(crstd, 1)

            pool.wait_ge(power_set, 1)
            for t in range(4):
                rest_linear(t, t % 2, KT)
            rest_cf(0)
            for m, u in pairs_of_steps(pool, 2, KT // 2):
                rest_linear(2 * m + u, u, KT)
            rows_power(0, 0)
            rest_cf(1)
            rows_power(1, 1)
            rest_cf(2)
            for m, u in pairs_of_steps(pool, 1, 3):
                cross_power(2 * m + u - 2)
                rest_cf(2 * m + u + 1)
            cross_power(4)
            rest_cf(7)
            cross_power(5)
            rest_linear(KT, 0, KT + 1)
            rest_linear(KT + 1, 1, KT + 1)
            cross_power(6)
            cross_power(7)
            for m, u in pairs_of_steps(pool, 5, 8):
                rest_linear(2 * m + u, u, KT + 1)
            rest_linear(16, 0, KT + 1)
            rows_power(2, 0)
            rows_power(3, 1)


def constants():
    freq = (1.0 / 10000.0 ** (np.arange(0, HD, 2, dtype=np.float32) / np.float32(HD))).astype(np.float32)
    angle = np.arange(S, dtype=np.float32)[None, :] * freq[:, None]
    sin, cos = np.sin(angle), np.cos(angle)
    rotary = np.concatenate([cos + sin, cos - sin] * 2, 0).astype(np.float32)
    causal = np.where(np.tril(np.ones((S, S), bool)), 0.0, MASKED).astype(np.float32)
    route = np.empty((RA, B + 1), np.float32)
    route[:, :B] = np.arange(B)
    route[:, B] = np.arange(RA) // R + 2
    return {"rotary": rotary, "causal": causal, "identity": np.eye(P, dtype=np.float32), "route": route}


def tiles(w):
    return w.reshape(KT, P, KT, P).transpose(2, 1, 0, 3)


def kernel(**inputs):
    import concourse.bacc as bacc
    from concourse.bass_utils import run_bass_kernel_spmd as run

    a = {k: np.asarray(v) for k, v in inputs.items()}
    x, ctx = a["x"], a["ctx_4096"]
    order = np.arange(D).reshape(D // HD, HD // 2, 2).transpose(0, 2, 1).reshape(-1)
    qkv = np.stack([tiles(a["L0_attn_Wq"][:, order]), tiles(a["L0_attn_Wk"][:, order]),
                    tiles(a["L0_attn_Wv"])], 1)
    ffn = np.zeros((KT + 1, P, KT + 1, P), np.float32)
    ffn[0, :, :KT, :RA] = a["L0_ffn_lora_A"].reshape(RA, KT, P).transpose(2, 1, 0)
    ffn[1:, :, :KT, :] = tiles(a["L0_ffn_weight"].T)
    ffn[1:, :RA, KT, :] = a["L0_ffn_lora_B"].transpose(0, 2, 1).reshape(RA, KT, P).transpose(1, 0, 2)
    ffn[1:, EXTRA:EXTRA + RA, KT, :] = ffn[1:, :RA, KT, :]
    ffn[1:, BIAS_ROW, KT, :] = a["L0_ffn_bias"].reshape(KT, P)
    ctx_feat = np.zeros((B, 2, P, KT // 2, LKP), np.float32)
    ctx_feat[..., :LK] = ctx.transpose(0, 2, 1).reshape(B, 2, KT // 2, P, LK).transpose(0, 1, 3, 2, 4)
    starts = a["L0_ffn_lora_start_indices"]
    arrays = {
        "x_feat": x.reshape(B * S, KT, P).transpose(2, 1, 0),
        "x_tok": x.transpose(1, 0, 2).reshape(S, B, KT, P),
        "qkv_w": qkv,
        "wo_w": tiles(a["L0_attn_Wo"]),
        "ffn_w": ffn,
        "ctx_feat": ctx_feat,
        "ctx_tok": ctx.reshape(B, CC, CR, D).transpose(0, 2, 1, 3),
        "starts": np.broadcast_to(starts[None, :], (RA, NA + 1)),
        **constants(),
    }
    arrays = {k: np.ascontiguousarray(v) for k, v in arrays.items()}
    nc = bacc.Bacc("TRN2", target_bir_lowering=False, num_devices=1)
    args = {k: nc.dram_tensor(k, v.shape, mybir.dt.from_np(v.dtype), kind="ExternalInput").ap()
            for k, v in arrays.items()}
    out = nc.dram_tensor("out", (B, S, D), F32, kind="ExternalOutput").ap()
    build(nc, out=out.rearrange("b s (k f) -> b s k f", k=KT), **args)
    r = run(nc, [arrays], core_ids=[0])
    return r.results[0]["out"]
```

```python
from contextlib import ExitStack

import numpy as np

import concourse.bass as bass
from concourse import mybir

F32 = mybir.dt.float32
F32R = mybir.dt.float32r
I32 = mybir.dt.int32
ALU = mybir.AluOpType
ACT = mybir.ActivationFunctionType
AX = mybir.AxisListType

P = 128
B = 8
S = 112
D = 1024
KT = D // P
HD = 64
PAIRS = D // (2 * HD)
HB = B // 2
HT = HB * S
LK = 375
LKP = LK + 1
CR = 125
CC = LK // CR
R = 16
NA = 3
RA = NA * R
BIAS_ROW = RA
SECOND = 64
EPS = 1e-5
MASKED = -2e9
WARM_UP = 6
SCORE_SCALE = 1.0 / (2.0 * HD ** 0.5)


def any_yet(n):
    return not isinstance(n, int) or n > 0


def pairs_of_steps(eng, first, last):
    with eng.Fori(first, last) as m:
        yield m, 0
        yield m, 1


def build(nc, x_feat, x_tok, qkv_w, wo_w, ffn_w, ctx_feat, ctx_tok, starts, rotary, causal,
          identity, route, out):
    st = ExitStack()
    with st:
        def sb(name, shape, dt=F32, scope=st):
            return scope.enter_context(nc.sbuf_tensor(name, shape, dt))

        def sem(name):
            return st.enter_context(nc.semaphore(name))

        with ExitStack() as early:
            x_raw = sb("x_raw", [P, KT, B * S], F32, early)
            w_mix0 = sb("w_mix0", [P, KT, P], F32, early)
        act_hi = sb("act_hi", [P, KT, B * S], F32R)
        act_lo = sb("act_lo", [P, KT, B * S], F32R)
        w_raw = [sb(f"w_raw{i}", [P, KT + 1, P]) for i in range(2)]
        w_hi = [sb(f"w_hi{i}", [P, KT + 1, P], F32R) for i in range(2)]
        w_lo = [sb(f"w_lo{i}", [P, KT + 1, P], F32R) for i in range(2)]
        y_feat = sb("y_feat", [P, 2, HT])
        ident = sb("ident", [P, P])
        mask = sb("mask", [S, S])
        turn = sb("turn", [P, S])
        stats = sb("stats", [S, B, KT, 6])
        mv = sb("mv", [S, B, 2])
        var_eps = sb("var_eps", [S, B])
        rstd = sb("rstd", [S, B, 1])
        centre = sb("centre", [S, B, 1])
        minus_half = sb("minus_half", [S, HB])
        route_c = sb("route_c", [RA, B + 1])
        starts_i = sb("starts_i", [RA, NA + 1], I32)
        starts_f = sb("starts_f", [RA, NA + 1])
        passed = sb("passed", [RA, NA + 1, B])
        sel = sb("sel", [RA, B])
        with ExitStack() as one:
            x_hi = sb("x_hi", [P, KT, B * S], F32R, one)
            x_lo = sb("x_lo", [P, KT, B * S], F32R, one)
            w_raw.append(sb("w_raw2", [P, KT, P], F32, one))
            w_hi.append(sb("w_hi2", [P, KT, P], F32R, one))
            w_lo.append(sb("w_lo2", [P, KT, P], F32R, one))
            w_mix = sb("w_mix", [P, KT, P], F32, one)
            qk = [[sb(f"{n}{i}", [P, B, S], F32, one) for n in ("q_feat", "k_feat")]
                  for i in range(2)]
            v_feat = sb("v_feat", [P, B, S], F32, one)
            v_tok = sb("v_tok", [S, B, P], F32, one)
            prob = [sb(f"prob{i}", [S, HB, S], F32, one) for i in range(4)]
            prob_t = [sb(f"prob_t{i}", [S, HB, S], F32, one) for i in range(4)]
            top = sb("top", [S, 4, HB], F32, one)
            shift = sb("shift", [S, 4, HB], F32, one)
            total = sb("total", [S, 4, HB], F32, one)
            inv = sb("inv", [S, 4, HB], F32, one)
        resid = sb("resid", [S, B, KT, P])
        with ExitStack() as three:
            x1 = sb("x1", [S, KT, P], F32, three)
            cf_raw = [sb(f"cf_raw{i}", [P, KT // 2, LKP], F32, three) for i in range(2)]
            cf_hi = sb("cf_hi", [P, KT, LKP], F32R, three)
            cf_lo = sb("cf_lo", [P, KT, LKP], F32R, three)
            ct = [sb(f"ctx_tok{i}", [CR, CC, D], F32, three) for i in range(2)]
            x2 = sb("x2", [S, KT, P], F32, three)
            x1_hi = sb("x1_hi", [P, KT, S], F32R, three)
            x1_lo = sb("x1_lo", [P, KT, S], F32R, three)
            cprob = sb("cprob", [S, LKP], F32, three)
            cprob_t = sb("cprob_t", [CR, CC, S], F32, three)
            ctop = sb("ctop", [S, 4], F32, three)
            stats2 = sb("stats2", [S, 2, 6], F32, three)
            mv2 = sb("mv2", [S, 4], F32, three)
        with ExitStack() as four:
            a_both = sb("a_both", [P, KT, P], F32R, four)
            t_raw = sb("t_raw", [RA, B, S], F32, four)
            t_part = sb("t_part", [RA, B, S], F32, four)
            t_cat = sb("t_cat", [P, B, S], F32R, four)
            end_raw = sb("end_raw", [P, 2, KT + 1, P], F32, four)
            end_hi = sb("end_hi", [P, 2, KT + 1, P], F32R, four)
            end_lo = sb("end_lo", [P, 2, KT + 1, P], F32R, four)

        bank = [st.enter_context(nc.psum_tensor(f"bank{i}", [P, 512], F32)) for i in range(8)]
        PROD = bank[0:2]
        TURN = bank[2:4]
        SCORE = bank[4:6]
        HEADS = bank[6]
        TURN2 = [bank[5], bank[7]]
        RANKS = [bank[2], bank[4]]
        ROWS = bank[4:8]

        const_in, warm_set = sem("const_in"), sem("warm_set")
        x_in = [sem(f"x_in{k}") for k in range(KT)]
        x_rounded, x_rest = sem("x_rounded"), sem("x_rest")
        w_in = [sem(f"w_in{i}") for i in range(3)]
        w0_mixed = [sem(f"w0_mixed{i}") for i in range(2)]
        w0_rounded = [sem(f"w0_rounded{i}") for i in range(3)]
        w0_rest = [sem(f"w0_rest{i}") for i in range(3)]
        w_mixed, w_rounded, w_rest = sem("w_mixed"), sem("w_rounded"), sem("w_rest")
        proj_done = sem("proj_done")
        qk_kept, v_kept = sem("qk_kept"), sem("v_kept")
        v_turned, v_tok_kept = sem("v_turned"), sem("v_tok_kept")
        scored, masked, topped, shifted = sem("scored"), sem("masked"), sem("topped"), sem("shifted")
        exped, inverted, normed = sem("exped"), sem("inverted"), sem("normed")
        prob_turned, prob_t_kept = sem("prob_turned"), sem("prob_t_kept")
        heads_done, heads_rounded = sem("heads_done"), sem("heads_rounded")
        heads_rest = sem("heads_rest")
        lin_in = [sem(f"lin_in{i}") for i in range(2)]
        lin_rounded, lin_rest, lin_done = sem("lin_rounded"), sem("lin_rest"), sem("lin_done")
        y_kept, y_turned, y_added = sem("y_kept"), sem("y_turned"), sem("y_added")
        y_stats = sem("y_stats")
        resid_in = sem("resid_in")
        power_set = sem("power_set")
        norm_aggr, norm_var, norm_rstd = sem("norm_aggr"), sem("norm_var"), sem("norm_rstd")
        x1_ready, x1_kept, x1_turned = sem("x1_ready"), sem("x1_kept"), sem("x1_turned")
        x1_rounded, x1_rest = sem("x1_rounded"), sem("x1_rest")
        cf_in = [sem(f"cf_in{i}") for i in range(2)]
        ct_in = [sem(f"ct_in{i}") for i in range(2)]
        cf_rounded, cf_rest = sem("cf_rounded"), sem("cf_rest")
        cscored, ctopped, cshifted = sem("cscored"), sem("ctopped"), sem("cshifted")
        cexped, cinverted, cnormed = sem("cexped"), sem("cinverted"), sem("cnormed")
        cturned, cprob_t_kept, cmixed = sem("cturned"), sem("cprob_t_kept"), sem("cmixed")
        cadded, cstats, caggr, cvar, crstd = (sem("cadded"), sem("cstats"), sem("caggr"),
                                              sem("cvar"), sem("crstd"))
        x2_ready, x2_kept, x2_turned = sem("x2_ready"), sem("x2_kept"), sem("x2_turned")
        x2_rounded, x2_rest = sem("x2_rounded"), sem("x2_rest")
        routed, t_filled, t_done = sem("routed"), sem("t_filled"), sem("t_done")
        t_masked, t_rounded, t_rest = sem("t_masked"), sem("t_rounded"), sem("t_rest")
        t_part_kept, t_added = sem("t_part_kept"), sem("t_added")
        end_in, end_rounded, end_rest = sem("end_in"), sem("end_rounded"), sem("end_rest")
        row_done, row_added, row_stats = sem("row_done"), sem("row_added"), sem("row_stats")
        row_aggr, row_var, row_rstd = sem("row_aggr"), sem("row_var"), sem("row_rstd")
        centred, out_ready, out_stored = sem("centred"), sem("out_ready"), sem("out_stored")
        last_ready = sem("last_ready")

        block = st.enter_context(nc.Block())

        BEGIN = [(0, 0), (1, 0), (0, 1), (1, 1)]
        END = [(KT - 2, 0), (KT - 1, 0), (KT - 2, 1), (KT - 1, 1)]
        NP = 2 * KT

        @block.sync
        def _(sp):
            sp.dma_start(w_raw[0][:, 0:KT, :], qkv_w[0, 0]).then_inc(w_in[0], 16)
            sp.dma_start(x_raw[:, 0, :], x_feat[:, 0, :]).then_inc(x_in[0], 16)
            sp.dma_start(w_raw[1][:, 0:KT, :], qkv_w[0, 1]).then_inc(w_in[1], 16)
            for k in range(1, KT):
                sp.dma_start(x_raw[:, k, :], x_feat[:, k, :]).then_inc(x_in[k], 16)
            sp.dma_start(w_raw[2][:, :, :], qkv_w[0, 2]).then_inc(w_in[2], 16)

            for w in range(2):
                sp.wait_ge(w0_mixed[w], 1)
                sp.dma_start(w_raw[w][:, 0:KT, :], qkv_w[1, w]).then_inc(w_in[w], 16)
            sp.wait_ge(w0_rest[2], 1)
            sp.dma_start(w_raw[2][:, :, :], qkv_w[1, 2]).then_inc(w_in[2], 16)
            with sp.Fori(2, PAIRS) as s:
                for w in range(2):
                    sp.wait_ge(w_mixed, 2 * (s - 2) + w + 1)
                    sp.dma_start(w_raw[w][:, 0:KT, :], qkv_w[s, w]).then_inc(w_in[w], 16)
                sp.wait_ge(w_rest, 3 * (s - 2) + 3)
                sp.dma_start(w_raw[2][:, :, :], qkv_w[s, 2]).then_inc(w_in[2], 16)

            for u in range(2):
                sp.wait_ge(w_mixed, 2 * (PAIRS - 2) + u + 1)
                sp.dma_start(w_raw[u][:, 0:KT, :], wo_w[u]).then_inc(lin_in[u], 16)
            sp.wait_ge(proj_done, 6 * PAIRS)
            sp.dma_start(resid[:, :, :, :], x_tok).then_inc(resid_in, 16)

            def load_linear(t, u, weights, tile, kt):
                sp.wait_ge(lin_rest, t - 1)
                sp.dma_start(w_raw[u][:, 0:kt, :], weights[tile]).then_inc(lin_in[u], 16)

            for u in range(2):
                load_linear(2 + u, u, wo_w, 2 + u, KT)
            sp.wait_ge(heads_rest, 2 * PAIRS)
            for c in range(2):
                sp.dma_start(cf_raw[c][:, :, :], ctx_feat[0, c]).then_inc(cf_in[c], 16)
            sp.dma_start(ct[0][:, :, :], ctx_tok[0]).then_inc(ct_in[0], 16)
            for m, u in pairs_of_steps(sp, 2, KT // 2):
                load_linear(2 * m + u, u, wo_w, 2 * m + u, KT)
            for u in range(2):
                load_linear(KT + u, u, ffn_w, u, KT + 1)
            with sp.Fori(1, B) as b:
                for c in range(2):
                    sp.wait_ge(cf_rest, 2 * (b - 1) + c + 1)
                    sp.dma_start(cf_raw[c][:, :, :], ctx_feat[b, c]).then_inc(cf_in[c], 16)
            for m, u in pairs_of_steps(sp, 5, 7):
                load_linear(2 * m + u, u, ffn_w, 2 * m + u - 8, KT + 1)
            sp.wait_ge(x2_rest, 2 * B)
            for i in range(2):
                sp.dma_start(end_raw[:, i, :, :], ffn_w[KT - 1 + i]).then_inc(end_in, 16)
            load_linear(14, 0, ffn_w, KT - 2, KT + 1)
            for b in range(B - 1):
                sp.wait_ge(out_ready, b + 1)
                sp.dma_start(out[b], resid[:, b, :, :]).then_inc(out_stored, 16)
            for i, ks in enumerate((slice(0, KT // 2), slice(KT // 2, KT))):
                sp.wait_ge(last_ready, i + 1)
                sp.dma_start(out[B - 1, :, ks, :], resid[:, B - 1, ks, :]).then_inc(out_stored, 16)
            sp.wait_ge(out_stored, 16 * (B + 1))

        @block.tensor
        def _(pe):
            def project_part(k, w, h, to):
                for a, b in ((w_hi[w], x_hi), (w_hi[w], x_lo), (w_lo[w], x_hi)):
                    last = pe.matmul(to[:, 0:HT], a[:, k, :], b[:, k, HT * h:HT * h + HT],
                                     start=(k == 0 and b is x_hi and a is w_hi[w]),
                                     stop=(k == KT - 1 and a is w_lo[w]))
                return last

            def project(w, h, to):
                for k in range(KT):
                    last = project_part(k, w, h, to)
                last.then_inc(proj_done, 1)

            def turn_v(s, h):
                pe.wait_ge(v_kept, 2 * s + h + 1)
                for b in range(HB):
                    last = pe.transpose(TURN[h][0:S, b * P:(b + 1) * P],
                                        v_feat[:, HB * h + b, :], ident[:, :])
                last.then_inc(v_turned, 1)

            def score(p, u, r):
                for b in range(HB):
                    for h in range(2):
                        rows = slice(HD * h, HD * h + HD)
                        last = pe.matmul(SCORE[h][0:S, b * S:(b + 1) * S],
                                         qk[u][0][rows, HB * r + b, :],
                                         qk[u][1][rows, HB * r + b, :], start=True, stop=True)
                        if b == HB - 1:
                            last.then_inc(scored, 1)

            def turn_prob(p, r):
                for h in range(2):
                    a = 2 * r + h
                    pe.wait_ge(normed, 4 * p + a + 1)
                    if r == 0 and (h == 0 or isinstance(p, int) and p == PAIRS - 1):
                        pe.wait_ge(v_tok_kept, 2 * p + 1)
                    elif r == 0:
                        pe.wait_ge(v_tok_kept, 2 * p + 2)
                    else:
                        pe.wait_ge(prob_t_kept, 4 * p + h + 1)
                        if h == 1:
                            pe.wait_ge(v_tok_kept, 2 * p + 2)
                    for b in range(HB):
                        last = pe.transpose(TURN[h][0:S, b * S:(b + 1) * S],
                                            prob[a][:, b, :], ident[0:S, 0:S])
                    last.then_inc(prob_turned, 1)

            def mix_heads(p, r):
                pe.wait_ge(prob_t_kept, 4 * p + 2 * r + 2)
                pe.wait_ge(v_tok_kept, 2 * p + r + 1)
                if any_yet(2 * p + r):
                    pe.wait_ge(heads_rest, 2 * p + r)
                for b in range(HB):
                    for h in range(2):
                        last = pe.matmul(HEADS[HD * h:HD * h + HD, b * S:(b + 1) * S],
                                         v_tok[:, HB * r + b, HD * h:HD * h + HD],
                                         prob_t[2 * r + h][:, b, :], start=True, stop=True)
                last.then_inc(heads_done, 1)

            def step(s, u):
                p, up = s - 1, 1 - u
                pe.wait_ge(w_rest, 3 * (s - 1) + 1)
                pe.wait_ge(v_kept, 2 * (s - 1) + 1)
                project(0, 0, PROD[0])
                if any_yet(4 * (p - 1) + 4):
                    pe.wait_ge(prob_t_kept, 4 * (p - 1) + 4)
                turn_v(p, 1)
                pe.wait_ge(qk_kept, 4 * p + 4)
                if any_yet(4 * p):
                    pe.wait_ge(masked, 4 * p)
                score(p, up, 0)
                pe.wait_ge(v_kept, 2 * (s - 1) + 2)
                project(0, 1, PROD[1])
                pe.wait_ge(masked, 4 * p + 2)
                score(p, up, 1)
                pe.wait_ge(w_rest, 3 * (s - 1) + 2)
                pe.wait_ge(qk_kept, 4 * s + 1)
                project(1, 0, PROD[0])
                turn_prob(p, 0)
                pe.wait_ge(qk_kept, 4 * s + 2)
                project(1, 1, PROD[1])
                mix_heads(p, 0)
                turn_prob(p, 1)
                pe.wait_ge(w_rest, 3 * (s - 1) + 3)
                pe.wait_ge(qk_kept, 4 * s + 3)
                project(2, 0, PROD[0])
                mix_heads(p, 1)
                pe.wait_ge(qk_kept, 4 * s + 4)
                project(2, 1, PROD[1])
                pe.wait_ge(prob_t_kept, 4 * p + 3)
                turn_v(s, 0)

            pe.wait_ge(warm_set, 1)
            for _ in range(WARM_UP):
                pe.matmul(bank[7][:, 0:HT], y_feat[:, 0, 0:P], y_feat[:, 0, :],
                          start=True, stop=True)

            for k, w in ([(k, 0) for k in range(4)] + [(k, 1) for k in range(4)]
                         + [(k, w) for k in range(4, KT) for w in range(2)]):
                if k == 0:
                    pe.wait_ge(w0_rest[w], 1)
                pe.wait_ge(x_rest, k + 1)
                for h in range(2):
                    last = project_part(k, w, h, (PROD, SCORE)[w][h])
                    if k == KT - 1:
                        last.then_inc(proj_done, 1)
            pe.wait_ge(w0_rest[2], 1)
            for h in range(2):
                pe.wait_ge(qk_kept, h + 1)
                project(2, h, PROD[h])
            pe.wait_ge(const_in, 16 * 5)
            turn_v(0, 0)
            step(1, 1)
            for m, u in pairs_of_steps(pe, 1, PAIRS // 2 - 1):
                step(2 * m + u, u)
            step(PAIRS - 2, 0)

            s, p = PAIRS - 1, PAIRS - 2
            pe.wait_ge(w_rest, 3 * (s - 1) + 1)
            pe.wait_ge(v_kept, 2 * (s - 1) + 1)
            project(0, 0, PROD[0])
            pe.wait_ge(prob_t_kept, 4 * (p - 1) + 4)
            turn_v(p, 1)
            pe.wait_ge(qk_kept, 4 * p + 4)
            pe.wait_ge(masked, 4 * p)
            score(p, 0, 0)
            pe.wait_ge(w_rest, 3 * (s - 1) + 2)
            pe.wait_ge(v_kept, 2 * (s - 1) + 2)
            project(1, 0, PROD[1])
            pe.wait_ge(masked, 4 * p + 2)
            score(p, 0, 1)
            pe.wait_ge(w_rest, 3 * (s - 1) + 3)
            pe.wait_ge(qk_kept, 4 * s + 1)
            project(2, 0, PROD[0])
            turn_prob(p, 0)
            pe.wait_ge(qk_kept, 4 * s + 2)
            pe.wait_ge(masked, 4 * p + 4)
            score(s, 1, 0)
            project(0, 1, PROD[1])
            mix_heads(p, 0)
            turn_prob(p, 1)
            pe.wait_ge(v_kept, 2 * s + 1)
            project(1, 1, PROD[0])
            mix_heads(p, 1)
            pe.wait_ge(prob_t_kept, 4 * p + 3)
            turn_v(s, 0)
            pe.wait_ge(qk_kept, 4 * s + 3)
            for k in range(KT):
                if k == 2:
                    turn_prob(s, 0)
                last = project_part(k, 2, 1, PROD[1])
            last.then_inc(proj_done, 1)
            pe.wait_ge(qk_kept, 4 * s + 4)
            pe.wait_ge(masked, 4 * s + 2)
            score(s, 1, 1)
            mix_heads(s, 0)
            pe.wait_ge(prob_t_kept, 4 * s + 2)
            turn_v(s, 1)

            def part(k, u, h, to, first, last_k):
                for w, x in ((w_hi[u], act_hi), (w_hi[u], act_lo), (w_lo[u], act_hi)):
                    last = pe.matmul(to[:, 0:HT], w[:, k, :], x[:, k, HT * h:HT * h + HT],
                                     start=(k == first and w is w_hi[u] and x is act_hi),
                                     stop=(k == last_k and w is w_lo[u]))
                return last

            def turn_y(n, i):
                pe.wait_ge(y_kept, n + 1)
                if any_yet(n - 1):
                    pe.wait_ge(y_added, n - 1)
                for b in range(HB):
                    last = pe.transpose(TURN[i][0:S, b * P:(b + 1) * P],
                                        y_feat[:, i, b * S:(b + 1) * S], ident[:, :])
                last.then_inc(y_turned, 1)

            def product(n, i, u, h, extra=False):
                if any_yet(n - 1):
                    pe.wait_ge(y_kept, n - 1)
                for k in range(KT):
                    if k == 2:
                        turn_y(n - 1, 1 - i)
                    last = part(k, u, h, PROD[i], 0, None if extra else KT - 1)
                if extra:
                    low_rank(i, u, h)
                else:
                    last.then_inc(lin_done, 1)

            def low_rank(i, u, h):
                rows = slice(HB * h, HB * h + HB)
                pe.matmul(PROD[i][:, 0:HT], w_hi[u][:, KT, :], t_cat[:, rows, :],
                          start=False, stop=False)
                pe.matmul(PROD[i][:, 0:HT], w_lo[u][0:SECOND, KT, :], t_cat[0:SECOND, rows, :],
                          start=False, stop=True).then_inc(lin_done, 1)

            for n, (j, h) in enumerate(BEGIN):
                if h == 0:
                    pe.wait_ge(lin_rest, j + 1)
                if n == 0:
                    pe.wait_ge(qk_kept, 4 * PAIRS)
                    pe.wait_ge(heads_rest, 2 * PAIRS - 2)
                    for k in range(KT - 1):
                        part(k, j, h, PROD[0], 0, None)
                    pe.wait_ge(heads_rest, 2 * PAIRS - 1)
                    part(KT - 1, j, h, PROD[0], 0, KT - 1).then_inc(lin_done, 1)
                elif n == 1:
                    pe.wait_ge(v_kept, 2 * PAIRS)
                    for k in range(KT):
                        if k == 2:
                            turn_prob(s, 1)
                        last = part(k, j, h, PROD[1], 0, KT - 1)
                    last.then_inc(lin_done, 1)
                    mix_heads(s, 1)
                    pe.wait_ge(prob_t_kept, 4 * PAIRS)
                    turn_y(0, 0)
                elif n == 2:
                    pe.wait_ge(y_kept, 1)
                    for k in range(KT - 1):
                        if k == 2:
                            turn_y(1, 1)
                        part(k, j, h, PROD[0], 0, None)
                    pe.wait_ge(heads_rest, 2 * PAIRS)
                    part(KT - 1, j, h, PROD[0], 0, KT - 1).then_inc(lin_done, 1)
                else:
                    product(n, 1, j, h)
            for m, u in pairs_of_steps(pe, 1, KT // 2 - 1):
                pe.wait_ge(lin_rest, 2 * m + u + 1)
                for h in range(2):
                    product(2 * (2 * m + u) + h, h, u, h)
            for n, (j, h) in enumerate(END, NP - 4):
                if h == 0:
                    pe.wait_ge(lin_rest, j + 1)
                if n < NP - 1:
                    product(n, n % 2, j % 2, h)

            def turn_x1(b, to):
                pe.wait_ge(x1_ready, b + 1)
                for c in range(2):
                    for k in range(4):
                        last = pe.transpose(to[c][:, k * S:(k + 1) * S], x1[:, 4 * c + k, :],
                                            ident[0:S, 0:S])
                    last.then_inc(x1_turned, 1)

            pe.wait_ge(y_kept, NP - 2)
            for k in range(KT - 2):
                if k == 2:
                    turn_y(NP - 2, 0)
                if k == 3:
                    turn_x1(0, TURN2)
                part(k, 1, 1, PROD[1], 0, None)

            def cross_score(b):
                pe.wait_ge(x1_rest, 2 * b + 2)
                if any_yet(b):
                    pe.wait_ge(cexped, b)
                for c in range(2):
                    pe.wait_ge(cf_rest, 2 * b + c + 1)
                    for k in range(4 * c, 4 * c + 4):
                        for w, x in ((x1_hi, cf_hi), (x1_hi, cf_lo), (x1_lo, cf_hi)):
                            last = pe.matmul(SCORE[0][0:S, 0:LKP], w[:, k, :], x[:, k, :],
                                             start=(k == 0 and w is x1_hi and x is cf_hi),
                                             stop=(k == KT - 1 and w is x1_lo))
                    last.then_inc(cscored, 1)

            def turn_x2(b):
                pe.wait_ge(x2_ready, b + 1)
                if any_yet(2 * b):
                    pe.wait_ge(x2_rest, 2 * b)
                for c in range(2):
                    for k in range(4):
                        last = pe.transpose(TURN2[c][:, k * S:(k + 1) * S], x2[:, 4 * c + k, :],
                                            ident[0:S, 0:S])
                    last.then_inc(x2_turned, 1)

            def cross_mix(b, u, m, between=lambda: None):
                pe.wait_ge(cprob_t_kept, b + 1)
                pe.wait_ge(ct_in[u], 16 * m + 16)
                if any_yet(2 * b):
                    pe.wait_ge(cadded, 2 * b)
                for n in range(2):
                    if n == 1:
                        between()
                    for c in range(CC):
                        last = pe.matmul(PROD[n][0:S, :], cprob_t[:, c, :],
                                         ct[u][:, c, 512 * n:512 * n + 512],
                                         start=(c == 0), stop=(c == CC - 1))
                    last.then_inc(cmixed, 1)

            def turn_cprob(b):
                pe.wait_ge(cnormed, b + 1)
                if any_yet(b):
                    pe.wait_ge(cprob_t_kept, b)
                for c in range(CC):
                    last = pe.transpose(HEADS[0:CR, c * S:(c + 1) * S],
                                        cprob[:, c * CR:(c + 1) * CR], ident[0:S, 0:S])
                last.then_inc(cturned, 1)

            def cross_step(b, u, m):
                known = isinstance(b, int)
                cross_score(b)
                if not known or b + 1 < B:
                    if known and b == 1:
                        pe.wait_ge(y_added, NP)
                    pe.wait_ge(x1_rest, 2 * b + 2)
                    turn_x1(b + 1, TURN)
                cross_mix(b - 1, 1 - u, m - 1 if u == 0 else m)
                if not known or b >= 2:
                    turn_x2(b - 2)
                turn_cprob(b)

            cross_score(0)
            turn_x1(1, TURN2)
            part(KT - 2, 1, 1, PROD[1], 0, None)
            part(KT - 1, 1, 1, PROD[1], 0, KT - 1).then_inc(lin_done, 1)
            turn_y(NP - 1, 1)
            turn_cprob(0)
            cross_step(1, 1, 0)
            for m, u in pairs_of_steps(pe, 1, 3):
                cross_step(2 * m + u, u, m)
            cross_step(6, 0, 3)
            cross_step(7, 1, 3)

            def lora(h):
                cols = slice(HT * h, HT * h + HT)
                to = RANKS[h]
                for k in range(KT):
                    if k == 0:
                        pe.matmul(to[:, 0:HT], a_both[:, k, :], act_hi[:, k, cols],
                                  start=True, stop=False)
                    pe.matmul(to[0:SECOND, 0:HT], a_both[:, k, 0:SECOND],
                              act_lo[:, k, cols], start=False, stop=False)
                    if k > 0:
                        last = pe.matmul(to[:, 0:HT], a_both[:, k, :], act_hi[:, k, cols],
                                         start=False, stop=(k == KT - 1))
                last.then_inc(t_done, 1)

            pe.wait_ge(lin_rest, KT + 1)
            lora(0)
            cross_mix(7, 1, 3, lambda: turn_x2(6))
            pe.wait_ge(lin_rest, KT + 2)
            pe.wait_ge(cadded, 2 * B - 1)
            for k in range(KT):
                part(k, 1, 0, PROD[0], 0, None)
            turn_x2(7)
            pe.wait_ge(t_rest, 1)
            low_rank(0, 1, 0)
            pe.wait_ge(lin_rest, KT + 3)
            pe.wait_ge(cadded, 2 * B)
            product(NP + 1, 1, 0, 0, extra=True)
            pe.wait_ge(x2_rest, 2 * B)
            lora(1)
            for n, u in ((NP + 2, 1), (NP + 3, 0)):
                pe.wait_ge(y_kept, n - 1)
                for k in range(KT):
                    if k == 2:
                        turn_y(n - 1, 1 - n % 2)
                    part(k, u, 1, PROD[n % 2], 0, None)
                pe.wait_ge(t_rest, 2)
                low_rank(n % 2, u, 1)
            for m, u in pairs_of_steps(pe, 6, 8):
                pe.wait_ge(lin_rest, 2 * m + u)
                for h in range(2):
                    product(NP + 2 * (2 * m + u - 10) + h, h, 1 - u, h, extra=True)
            pe.wait_ge(end_rest, 2)
            for b in range(B):
                to, tok = ROWS[b % 4][0:S, 0:2 * P], slice(b * S, b * S + S)
                if b >= 4:
                    pe.wait_ge(row_added, b - 3)
                for k in range(KT):
                    if b == 0 and k == 3:
                        turn_y(2 * NP - 5, 1)
                    for x, w in ((act_hi, end_hi), (act_hi, end_lo), (act_lo, end_hi)):
                        pe.matmul(to, x[:, k, tok], w[:, :, k, :],
                                  start=(k == 0 and x is act_hi and w is end_hi), stop=False)
                pe.matmul(to, t_cat[0:SECOND, b, :], end_lo[0:SECOND, :, KT, :],
                          start=False, stop=False)
                pe.matmul(to, t_cat[:, b, :], end_hi[:, :, KT, :],
                          start=False, stop=True).then_inc(row_done, 1)

        @block.scalar
        def _(act):
            act.dma_start(turn[:, :], rotary).then_inc(const_in, 16)
            act.dma_start(ident[:, :], identity).then_inc(const_in, 16)
            act.dma_start(mask[:, :], causal).then_inc(const_in, 16)
            act.dma_start(route_c[:, :], route).then_inc(const_in, 16)
            act.dma_start(starts_i[:, :], starts).then_inc(const_in, 16)

            def round_w(s, w):
                if w < 2:
                    act.wait_ge(w_mixed, 2 * (s - 1) + w + 1)
                else:
                    act.wait_ge(w_in[2], 16 * s + 16)
                act.wait_ge(proj_done, 6 * (s - 1) + 2 * w + 2)
                src = w_mix if w < 2 else w_raw[2]
                act.activation(w_hi[w][:, 0:KT, :], src[:, :, :], ACT.Copy).then_inc(w_rounded, 1)

            def keep_v(s, h, done, frm):
                act.wait_ge(proj_done, done)
                if any_yet(2 * (s - 1) + h + 1):
                    act.wait_ge(v_turned, 2 * (s - 1) + h + 1)
                act.activation(v_feat[:, HB * h:HB * h + HB, :], frm[:, 0:HT],
                               ACT.Copy).then_inc(v_kept, 1)

            def keep_v_tok(s, h):
                act.wait_ge(v_turned, 2 * s + h + 1)
                act.activation(v_tok[:, HB * h:HB * h + HB, :], TURN[h][0:S, :],
                               ACT.Copy).then_inc(v_tok_kept, 1)

            def exponentials(p, r):
                for h in range(2):
                    a = 2 * r + h
                    act.wait_ge(shifted, 4 * p + a + 1)
                    for b in range(HB):
                        last = act.activation(prob[a][:, b, :], prob[a][:, b, :], ACT.Exp,
                                              bias=shift[:, a, b:b + 1], scale=SCORE_SCALE,
                                              accum_out=total[:, a, b:b + 1])
                    last.then_inc(exped, 1)

            def keep_prob_t(p, r):
                for h in range(2):
                    a = 2 * r + h
                    act.wait_ge(prob_turned, 4 * p + a + 1)
                    if any_yet(2 * (p - 1) + r + 1):
                        act.wait_ge(heads_done, 2 * (p - 1) + r + 1)
                    act.activation(prob_t[a][:, :, :], TURN[h][0:S, 0:HT],
                                   ACT.Copy).then_inc(prob_t_kept, 1)

            def round_heads(p, r):
                act.wait_ge(heads_done, 2 * p + r + 1)
                act.activation(act_hi[:, p, HT * r:HT * r + HT], HEADS[:, 0:HT],
                               ACT.Copy).then_inc(heads_rounded, 1)

            def step(s):
                p = s - 1
                round_w(s, 2)
                keep_v_tok(p, 1)
                exponentials(p, 0)
                round_w(s + 1, 0)
                exponentials(p, 1)
                keep_prob_t(p, 0)
                round_w(s + 1, 1)
                round_heads(p, 0)
                keep_prob_t(p, 1)
                keep_v(s, 0, 6 * s + 5, PROD[0])
                round_heads(p, 1)
                keep_v(s, 1, 6 * s + 6, PROD[1])
                keep_v_tok(s, 0)

            def round_x(k):
                act.wait_ge(x_in[k], 16)
                act.activation(x_hi[:, k, :], x_raw[:, k, :], ACT.Copy).then_inc(x_rounded, 1)

            act.wait_ge(w0_mixed[0], 1)
            act.activation(w_hi[0][:, 0:KT, :], w_mix0[:, :, :], ACT.Copy).then_inc(w0_rounded[0], 1)
            round_x(0)
            round_x(1)
            act.wait_ge(w0_mixed[1], 1)
            act.activation(w_hi[1][:, 0:KT, :], w_mix[:, :, :], ACT.Copy).then_inc(w0_rounded[1], 1)
            for k in range(2, KT):
                round_x(k)
            act.wait_ge(w_in[2], 16)
            act.activation(w_hi[2][:, :, :], w_raw[2][:, :, :], ACT.Copy).then_inc(w0_rounded[2], 1)
            round_w(1, 0)
            round_w(1, 1)
            keep_v(0, 0, 5, PROD[0])
            keep_v(0, 1, 6, PROD[1])
            keep_v_tok(0, 0)
            step(1)
            for m, u in pairs_of_steps(act, 1, PAIRS // 2 - 1):
                step(2 * m + u)
            step(PAIRS - 2)

            def round_linear(t, u, kt, arrived):
                act.wait_ge(lin_in[u], 16 * arrived)
                act.activation(w_hi[u][:, 0:kt, :], w_raw[u][:, 0:kt, :],
                               ACT.Copy).then_inc(lin_rounded, 1)

            def keep_y(n, i):
                act.wait_ge(lin_done, n + 1)
                if any_yet(n - 1):
                    act.wait_ge(y_turned, n - 1)
                act.activation(y_feat[:, i, :], PROD[i][:, 0:HT], ACT.Copy).then_inc(y_kept, 1)

            s, p = PAIRS - 1, PAIRS - 2
            round_w(s, 2)
            keep_v_tok(p, 1)
            exponentials(p, 0)
            exponentials(p, 1)
            keep_v(s, 0, 6 * s + 3, PROD[0])
            keep_prob_t(p, 0)
            exponentials(s, 0)
            act.wait_ge(proj_done, 6 * s + 4)
            round_linear(0, 0, KT, 1)
            round_heads(p, 0)
            keep_prob_t(p, 1)
            act.wait_ge(proj_done, 6 * s + 5)
            round_linear(1, 1, KT, 1)
            round_heads(p, 1)
            keep_v_tok(s, 0)
            keep_prob_t(s, 0)
            keep_v(s, 1, 6 * s + 6, PROD[1])
            round_heads(s, 0)
            keep_v_tok(s, 1)
            exponentials(s, 1)
            keep_prob_t(s, 1)
            keep_y(0, 0)
            round_heads(s, 1)
            keep_y(1, 1)
            keep_y(2, 0)
            round_linear(2, 0, KT, 2)
            keep_y(3, 1)
            round_linear(3, 1, KT, 2)

            def round_cf(b, c):
                act.wait_ge(cf_in[c], 16 * b + 16)
                if any_yet(2 * (b - 1) + c + 1):
                    act.wait_ge(cscored, 2 * (b - 1) + c + 1)
                act.activation(cf_hi[:, 4 * c:4 * c + 4, :], cf_raw[c][:, :, :],
                               ACT.Copy).then_inc(cf_rounded, 1)

            round_cf(0, 0)
            round_cf(0, 1)
            for m, u in pairs_of_steps(act, 1, KT // 2 - 1):
                keep_y(2 * (2 * m + u), 0)
                keep_y(2 * (2 * m + u) + 1, 1)
                round_linear(2 * m + u + 2, u, KT, m + 2)

            def keep_x1(b):
                act.wait_ge(x1_ready, b + 1)
                act.activation(resid[:, b, :, :], x1[:, :, :], ACT.Copy).then_inc(x1_kept, 1)

            def round_x1(b, frm):
                for c in range(2):
                    act.wait_ge(x1_turned, 2 * b + c + 1)
                    if any_yet(2 * b):
                        act.wait_ge(cscored, 2 * b)
                    act.activation(x1_hi[:, 4 * c:4 * c + 4, :], frm[c][:, 0:4 * S],
                                   ACT.Copy).then_inc(x1_rounded, 1)

            def round_x2(b):
                for c in range(2):
                    act.wait_ge(x2_turned, 2 * b + c + 1)
                    to = act_hi[:, :, :].rearrange("p k (b s) -> p k b s", b=B)
                    act.activation(to[:, 4 * c:4 * c + 4, b, :], TURN2[c][:, 0:4 * S],
                                   ACT.Copy).then_inc(x2_rounded, 1)

            def keep_x2(b):
                act.wait_ge(x2_ready, b + 1)
                act.activation(resid[:, b, :, :], x2[:, :, :], ACT.Copy).then_inc(x2_kept, 1)

            def cross_step(b, u):
                known = isinstance(b, int)
                first, second = known and b == 0, known and b == 1
                if not known or b + 1 < B:
                    round_cf(b + 1, 0)
                    if not first:
                        round_x1(b + 1, TURN)
                    if not second:
                        round_cf(b + 1, 1)
                act.wait_ge(cshifted, b + 1)
                act.activation(cprob[:, 0:LK], SCORE[0][0:S, 0:LK], ACT.Exp,
                               bias=ctop[:, 1:2], accum_out=ctop[:, 2:3]).then_inc(cexped, 1)
                if first:
                    round_x1(1, TURN2)
                    keep_y(NP - 1, 1)
                if second:
                    round_cf(2, 1)
                if any_yet(b):
                    act.dma_start(ct[u][:, :, :], ctx_tok[b]).then_inc(ct_in[u], 16)
                if not known or b >= 2:
                    keep_x2(b - 2)
                    round_x2(b - 2)
                act.wait_ge(cturned, b + 1)
                if any_yet(b):
                    act.wait_ge(cmixed, 2 * b)
                act.activation(cprob_t[:, :, :], HEADS[0:CR, 0:CC * S],
                               ACT.Copy).then_inc(cprob_t_kept, 1)
                if not known or b + 2 < B:
                    keep_x1(b + 2)

            def keep_t_part(h):
                rows = slice(HB * h, HB * h + HB)
                act.wait_ge(t_done, h + 1)
                act.activation(t_part[:, rows, :],
                               RANKS[h][SECOND:SECOND + RA, 0:HT].rearrange("p (b s) -> p b s", b=HB),
                               ACT.Copy).then_inc(t_part_kept, 1)

            for n in range(NP - 4, NP - 1):
                keep_y(n, n % 2)
            keep_x1(0)
            round_x1(0, TURN2)
            keep_x1(1)
            cross_step(0, 0)
            cross_step(1, 1)
            for m, u in pairs_of_steps(act, 1, 3):
                cross_step(2 * m + u, u)
            cross_step(6, 0)
            act.wait_ge(lin_in[0], 16 * 5)
            act.wait_ge(x1_turned, 2 * B)
            act.activation(a_both[:, :, :], w_raw[0][:, 0:KT, :],
                           ACT.Copy).then_inc(lin_rounded, 1)
            round_linear(KT + 1, 1, KT + 1, 5)
            cross_step(7, 1)
            round_linear(KT + 2, 0, KT + 1, 6)
            keep_x2(6)
            keep_t_part(0)
            round_x2(6)

            def round_t(h):
                rows = slice(HB * h, HB * h + HB)
                act.wait_ge(t_masked, h + 1)
                act.wait_ge(t_filled, 2)
                act.activation(t_cat[0:RA, rows, :], t_raw[:, rows, :],
                               ACT.Copy).then_inc(t_rounded, 1)

            round_t(0)
            keep_x2(7)
            round_x2(7)
            keep_y(NP, 0)
            keep_y(NP + 1, 1)
            keep_t_part(1)
            round_t(1)
            for h in range(2):
                keep_y(NP + 2 + h, h)
                round_linear(11 + h, 1 - h, KT + 1, 6 + h)
            for u in range(2):
                keep_y(NP + 4 + 2 * u, 0)
                keep_y(NP + 5 + 2 * u, 1)
                round_linear(13 + u, 1 - u, KT + 1, 7 + u)
            act.wait_ge(end_in, 32)
            for i in range(2):
                act.activation(end_hi[:, i, :, :], end_raw[:, i, :, :],
                               ACT.Copy).then_inc(end_rounded, 1)
            for u in range(2):
                keep_y(NP + 8 + 2 * u, 0)
                keep_y(NP + 9 + 2 * u, 1)
            for b in range(B - 1):
                act.wait_ge(centred, b + 1)
                act.activation(resid[:, b, :, :], resid[:, b, :, :], ACT.Identity,
                               bias=centre[:, b, :], scale=rstd[:, b, :]).then_inc(out_ready, 1)

        @block.vector
        def _(dve):
            dve.memset(y_feat[:, 0, :], 1.0).then_inc(warm_set, 1)
            dve.wait_ge(w_in[0], 16)
            raw = w_raw[0][:, 0:KT, :].rearrange("p k (h t i) -> p (k h) t i", h=2, t=2)
            mix = w_mix0[:, :, :].rearrange("p k (h t i) -> p (k h) t i", h=2, t=2)
            dve.tensor_tensor(mix[:, :, 0, :], raw[:, :, 0, :], raw[:, :, 1, :], ALU.add)
            dve.tensor_tensor(mix[:, :, 1, :], raw[:, :, 0, :], raw[:, :, 1, :],
                              ALU.subtract).then_inc(w0_mixed[0], 1)
            dve.wait_ge(w0_rounded[0], 1)
            dve.tensor_tensor(w_lo[0][:, 0:KT, :], w_mix0[:, :, :],
                              w_hi[0][:, 0:KT, :].bitcast(F32), ALU.subtract).then_inc(w0_rest[0], 1)
            for k in range(KT):
                dve.wait_ge(x_rounded, k + 1)
                dve.tensor_tensor(x_lo[:, k, :], x_raw[:, k, :], x_hi[:, k, :].bitcast(F32),
                                  ALU.subtract).then_inc(x_rest, 1)
            dve.wait_ge(w0_rounded[2], 1)
            dve.tensor_tensor(w_lo[2][:, :, :], w_raw[2][:, :, :],
                              w_hi[2][:, :, :].bitcast(F32), ALU.subtract).then_inc(w0_rest[2], 1)

            dve.wait_ge(const_in, 16 * 5)
            dve.tensor_copy(starts_f[:, :], starts_i[:, :]).then_inc(routed, 1)
            dve.wait_ge(routed, 1)
            for i in range(NA + 1):
                dve.tensor_scalar(passed[:, i, :], route_c[:, 0:B], starts_f[:, i:i + 1], None,
                                  ALU.is_ge).then_inc(routed, 1)
            for i in range(1, NA + 1):
                dve.wait_ge(routed, 4 + i)
                dve.tensor_tensor(passed[:, 0, :], passed[:, 0, :], passed[:, i, :],
                                  ALU.add).then_inc(routed, 1)
            dve.wait_ge(routed, 5 + NA)
            dve.tensor_scalar(sel[:, :], passed[:, 0, :], route_c[:, B:B + 1], None,
                              ALU.is_equal).then_inc(routed, 1)

            scale = turn[:, :].unsqueeze(1).broadcast_to([P, HB, S])
            hidden = mask[:, :].unsqueeze(1).broadcast_to([S, HB, S])

            def keep_qk(u, w, h, done, frm):
                dve.wait_ge(proj_done, done)
                dve.tensor_tensor(qk[u][w][:, HB * h:HB * h + HB, :],
                                  frm[:, 0:HT].rearrange("p (b s) -> p b s", b=HB),
                                  scale, ALU.mult).then_inc(qk_kept, 1)

            def mask_and_top(p, r):
                for h in range(2):
                    a = 2 * r + h
                    dve.wait_ge(scored, 4 * p + a + 1)
                    if any_yet(4 * (p - 1) + a + 1):
                        dve.wait_ge(prob_turned, 4 * (p - 1) + a + 1)
                    dve.tensor_tensor(prob[a][:, :, :],
                                      SCORE[h][0:S, 0:HT].rearrange("p (b s) -> p b s", b=HB),
                                      hidden, ALU.add).then_inc(masked, 1)
                for h in range(2):
                    a = 2 * r + h
                    dve.wait_ge(masked, 4 * p + a + 1)
                    dve.tensor_reduce(top[:, a, :], prob[a][:, :, :], AX.X,
                                      ALU.max).then_inc(topped, 1)
                for h in range(2):
                    a = 2 * r + h
                    dve.wait_ge(topped, 4 * p + a + 1)
                    dve.tensor_scalar(shift[:, a, :], top[:, a, :], -SCORE_SCALE, None,
                                      ALU.mult).then_inc(shifted, 1)

            def normalise(p, r):
                for h in range(2):
                    a = 2 * r + h
                    dve.wait_ge(exped, 4 * p + a + 1)
                    dve.reciprocal(inv[:, a, :], total[:, a, :]).then_inc(inverted, 1)
                for h in range(2):
                    a = 2 * r + h
                    dve.wait_ge(inverted, 4 * p + a + 1)
                    dve.tensor_tensor(prob[a][:, :, :], prob[a][:, :, :],
                                      inv[:, a, :].unsqueeze(2).broadcast_to([S, HB, S]),
                                      ALU.mult).then_inc(normed, 1)

            def rest_heads(p, r):
                dve.wait_ge(heads_rounded, 2 * p + r + 1)
                dve.tensor_tensor(act_lo[:, p, HT * r:HT * r + HT], HEADS[:, 0:HT],
                                  act_hi[:, p, HT * r:HT * r + HT].bitcast(F32),
                                  ALU.subtract).then_inc(heads_rest, 1)

            def step(s, u):
                p = s - 1
                if any_yet(4 * (s - 1)):
                    dve.wait_ge(scored, 4 * (s - 1))
                keep_qk(u, 0, 0, 6 * s + 1, PROD[0])
                mask_and_top(p, 0)
                keep_qk(u, 0, 1, 6 * s + 2, PROD[1])
                normalise(p, 0)
                mask_and_top(p, 1)
                keep_qk(u, 1, 0, 6 * s + 3, PROD[0])
                normalise(p, 1)
                keep_qk(u, 1, 1, 6 * s + 4, PROD[1])
                rest_heads(p, 0)
                rest_heads(p, 1)

            for w in range(2):
                for h in range(2):
                    keep_qk(0, w, h, 2 * w + h + 1, (PROD, SCORE)[w][h])
            step(1, 1)
            for m, u in pairs_of_steps(dve, 1, PAIRS // 2 - 1):
                step(2 * m + u, u)
            step(PAIRS - 2, 0)

            s, p = PAIRS - 1, PAIRS - 2
            dve.wait_ge(scored, 4 * (s - 1))
            keep_qk(1, 0, 0, 6 * s + 1, PROD[0])
            mask_and_top(p, 0)
            keep_qk(1, 1, 0, 6 * s + 2, PROD[1])
            normalise(p, 0)
            mask_and_top(p, 1)
            normalise(p, 1)
            mask_and_top(s, 0)
            keep_qk(1, 0, 1, 6 * s + 4, PROD[1])
            normalise(s, 0)
            rest_heads(p, 0)
            keep_qk(1, 1, 1, 6 * s + 5, PROD[0])
            rest_heads(p, 1)
            mask_and_top(s, 1)
            rest_heads(s, 0)
            normalise(s, 1)
            rest_heads(s, 1)

            def add_y(n, i, j, h):
                rows = slice(HB * h, HB * h + HB)
                dve.wait_ge(y_turned, n + 1)
                dve.tensor_tensor(resid[:, rows, j, :],
                                  TURN[i][0:S, :].rearrange("p (b s) -> p b s", b=HB),
                                  resid[:, rows, j, :], ALU.add).then_inc(y_added, 1)
                dve.wait_ge(y_added, n + 1)
                for b in range(HB * h, HB * h + HB):
                    last = dve.bn_stats(stats[:, b, j, :], resid[:, b, j, :])
                last.then_inc(y_stats, 1)

            def row_norms(q, n, h):
                rows = slice(HB * h, HB * h + HB)
                dve.wait_ge(y_stats, n + 1)
                for b in range(HB * h, HB * h + HB):
                    last = dve.bn_aggr(mv[:, b, :], stats[:, b, :, :])
                last.then_inc(norm_aggr, 1)
                dve.wait_ge(norm_aggr, q + 1)
                dve.tensor_scalar(var_eps[:, rows], mv[:, rows, 1], EPS, None,
                                  ALU.add).then_inc(norm_var, 1)

            dve.wait_ge(resid_in, 16)
            for n, (j, h) in enumerate(BEGIN):
                add_y(n, n % 2, j, h)
            for m, u in pairs_of_steps(dve, 1, KT // 2 - 1):
                for h in range(2):
                    add_y(2 * (2 * m + u) + h, h, 2 * m + u, h)

            def norm_x1(b):
                if any_yet(b):
                    dve.wait_ge(x1_turned, 2 * b)
                    dve.wait_ge(x1_kept, b)
                dve.tensor_scalar(x1[:, :, :], resid[:, b, :, :], mv[:, b, 0:1], rstd[:, b, :],
                                  ALU.subtract, ALU.mult).then_inc(x1_ready, 1)

            def rest_x1(b, frm):
                for c in range(2):
                    dve.wait_ge(x1_rounded, 2 * b + c + 1)
                    dve.tensor_tensor(x1_lo[:, 4 * c:4 * c + 4, :],
                                      frm[c][:, 0:4 * S].rearrange("p (k s) -> p k s", k=4),
                                      x1_hi[:, 4 * c:4 * c + 4, :].bitcast(F32),
                                      ALU.subtract).then_inc(x1_rest, 1)

            def rest_x2(b):
                lo = act_lo[:, :, :].rearrange("p k (b s) -> p k b s", b=B)
                hi = act_hi[:, :, :].bitcast(F32).rearrange("p k (b s) -> p k b s", b=B)
                for c in range(2):
                    ks = slice(4 * c, 4 * c + 4)
                    dve.wait_ge(x2_rounded, 2 * b + c + 1)
                    dve.tensor_tensor(lo[:, ks, b, :],
                                      TURN2[c][:, 0:4 * S].rearrange("p (k s) -> p k s", k=4),
                                      hi[:, ks, b, :], ALU.subtract).then_inc(x2_rest, 1)

            def sum_x2(b):
                if any_yet(b):
                    dve.wait_ge(x2_turned, 2 * b)
                    dve.wait_ge(x2_kept, b)
                dve.wait_ge(x1_kept, b + 1)
                for n in range(2):
                    ks = slice(4 * n, 4 * n + 4)
                    dve.wait_ge(cmixed, 2 * b + n + 1)
                    dve.tensor_tensor(x2[:, ks, :],
                                      PROD[n][0:S, :].rearrange("p (k s) -> p k s", k=4),
                                      resid[:, b, ks, :], ALU.add).then_inc(cadded, 1)
                for n in range(2):
                    dve.wait_ge(cadded, 2 * b + n + 1)
                    last = dve.bn_stats(stats2[:, n, :], x2[:, 4 * n:4 * n + 4, :])
                last.then_inc(cstats, 1)
                dve.wait_ge(const_in, 16 * 5)
                dve.wait_ge(cstats, b + 1)
                dve.bn_aggr(mv2[:, 0:2], stats2[:, :, :]).then_inc(caggr, 1)
                dve.wait_ge(caggr, b + 1)
                dve.tensor_scalar(mv2[:, 2:3], mv2[:, 1:2], EPS, None, ALU.add).then_inc(cvar, 1)

            def norm_x2(b):
                dve.wait_ge(crstd, b + 1)
                dve.tensor_scalar(x2[:, :, :], x2[:, :, :], mv2[:, 0:1], mv2[:, 3:4],
                                  ALU.subtract, ALU.mult).then_inc(x2_ready, 1)

            def cross_step(b):
                known = isinstance(b, int)
                if not known or b >= 2:
                    sum_x2(b - 2)
                dve.wait_ge(cscored, 2 * b + 2)
                if any_yet(b):
                    dve.wait_ge(cturned, b)
                dve.tensor_reduce(ctop[:, 0:1], SCORE[0][0:S, 0:LK], AX.X,
                                  ALU.max).then_inc(ctopped, 1)
                dve.wait_ge(ctopped, b + 1)
                dve.tensor_scalar(ctop[:, 1:2], ctop[:, 0:1], -1.0, None,
                                  ALU.mult).then_inc(cshifted, 1)
                if not known or b >= 2:
                    norm_x2(b - 2)
                if not known or b + 1 < B:
                    rest_x1(b + 1, TURN2 if known and b == 0 else TURN)
                dve.wait_ge(cexped, b + 1)
                dve.reciprocal(ctop[:, 3:4], ctop[:, 2:3]).then_inc(cinverted, 1)
                dve.wait_ge(cinverted, b + 1)
                dve.tensor_scalar(cprob[:, 0:LK], cprob[:, 0:LK], ctop[:, 3:4], None,
                                  ALU.mult).then_inc(cnormed, 1)
                if not known or b + 2 < B:
                    norm_x1(b + 2)
                if known and b == 0:
                    add_y(NP - 1, 1, KT - 1, 1)
                    row_norms(1, NP - 1, 1)
                if not known or b >= 2:
                    rest_x2(b - 2)

            add_y(NP - 4, 0, KT - 2, 0)
            add_y(NP - 3, 1, KT - 1, 0)
            row_norms(0, NP - 3, 0)
            dve.wait_ge(norm_rstd, 1)
            norm_x1(0)
            add_y(NP - 2, 0, KT - 2, 1)
            rest_x1(0, TURN2)
            norm_x1(1)
            cross_step(0)
            cross_step(1)
            dve.wait_ge(norm_rstd, 2)
            for m, u in pairs_of_steps(dve, 1, 3):
                cross_step(2 * m + u)
            cross_step(6)
            cross_step(7)

            def mask_t(h):
                rows = slice(HB * h, HB * h + HB)
                dve.wait_ge(t_part_kept, h + 1)
                dve.tensor_tensor(t_part[:, rows, :],
                                  RANKS[h][0:RA, 0:HT].rearrange("p (b s) -> p b s", b=HB),
                                  t_part[:, rows, :], ALU.add).then_inc(t_added, 1)
                dve.wait_ge(t_added, h + 1)
                dve.tensor_tensor(t_raw[:, rows, :], t_part[:, rows, :],
                                  sel[:, rows].unsqueeze(2).broadcast_to([RA, HB, S]),
                                  ALU.mult).then_inc(t_masked, 1)

            def rest_t(h):
                rows = slice(HB * h, HB * h + HB)
                dve.wait_ge(t_rounded, h + 1)
                dve.tensor_tensor(t_cat[SECOND:SECOND + RA, rows, :], t_raw[:, rows, :],
                                  t_cat[0:RA, rows, :].bitcast(F32),
                                  ALU.subtract).then_inc(t_rest, 1)

            sum_x2(6)
            norm_x2(6)
            dve.wait_ge(cf_rest, 2 * B)
            dve.memset(t_cat[32:SECOND, :, :].bitcast(F32), 1.0).then_inc(t_filled, 1)
            dve.memset(t_cat[SECOND:P, :, :].bitcast(F32), 0.0).then_inc(t_filled, 1)
            dve.wait_ge(t_filled, 2)
            mask_t(0)
            sum_x2(7)
            rest_x2(6)
            norm_x2(7)
            rest_t(0)
            rest_x2(7)
            add_y(NP, 0, 0, 0)
            mask_t(1)
            rest_t(1)
            add_y(NP + 1, 1, 1, 0)
            add_y(NP + 2, 0, 0, 1)
            add_y(NP + 3, 1, 1, 1)
            for m, u in pairs_of_steps(dve, 1, 3):
                for h in range(2):
                    add_y(NP + 2 * (2 * m + u) + h, h, 2 * m + u, h)

            for b in range(B):
                dve.wait_ge(row_done, b + 1)
                dve.tensor_tensor(resid[:, b, KT - 2:KT, :],
                                  ROWS[b % 4][0:S, 0:2 * P].rearrange("p (k f) -> p k f", k=2),
                                  resid[:, b, KT - 2:KT, :], ALU.add).then_inc(row_added, 1)
                dve.wait_ge(row_added, b + 1)
                for j in range(KT - 2, KT):
                    last = dve.bn_stats(stats[:, b, j, :], resid[:, b, j, :])
                last.then_inc(row_stats, 1)
                dve.wait_ge(row_stats, b + 1)
                dve.bn_aggr(mv[:, b, :], stats[:, b, :, :]).then_inc(row_aggr, 1)
                dve.wait_ge(row_aggr, b + 1)
                dve.tensor_scalar(var_eps[:, b:b + 1], mv[:, b, 1:2], EPS, None,
                                  ALU.add).then_inc(row_var, 1)
                dve.wait_ge(row_rstd, b + 1)
                if b < B - 1:
                    dve.scalar_tensor_tensor(out=centre[:, b, :], in0=mv[:, b, 0:1],
                                             scalar=-1.0, in1=rstd[:, b, :], op0=ALU.mult,
                                             op1=ALU.mult).then_inc(centred, 1)
                else:
                    for ks in (slice(0, KT // 2), slice(KT // 2, KT)):
                        dve.tensor_scalar(resid[:, b, ks, :], resid[:, b, ks, :], mv[:, b, 0:1],
                                          rstd[:, b, :], ALU.subtract,
                                          ALU.mult).then_inc(last_ready, 1)

        @block.gpsimd
        def _(pool):
            pool.memset(minus_half[:, :], -0.5).then_inc(power_set, 1)

            def mix_w(w):
                raw = w_raw[w][:, 0:KT, :].rearrange("p k (h t i) -> p (k h) t i", h=2, t=2)
                mix = w_mix[:, :, :].rearrange("p k (h t i) -> p (k h) t i", h=2, t=2)
                pool.tensor_tensor(mix[:, :, 0, :], raw[:, :, 0, :], raw[:, :, 1, :], ALU.add)
                return pool.tensor_tensor(mix[:, :, 1, :], raw[:, :, 0, :], raw[:, :, 1, :],
                                          ALU.subtract)

            def rest_w(w):
                src = w_mix if w < 2 else w_raw[2]
                return pool.tensor_tensor(w_lo[w][:, 0:KT, :], src[:, :, :],
                                          w_hi[w][:, 0:KT, :].bitcast(F32), ALU.subtract)

            def prepare_w(s):
                for w in range(2):
                    pool.wait_ge(w_in[w], 16 * s + 16)
                    if any_yet(3 * (s - 2) + w + 2 if w == 0 else 3 * (s - 1) + 1):
                        pool.wait_ge(w_rest, 3 * (s - 2) + 2 if w == 0 else 3 * (s - 1) + 1)
                    mix_w(w).then_inc(w_mixed, 1)
                    pool.wait_ge(w_rounded, 3 * (s - 1) + w + 1)
                    rest_w(w).then_inc(w_rest, 1)
                pool.wait_ge(w_rounded, 3 * (s - 1) + 3)
                rest_w(2).then_inc(w_rest, 1)

            pool.wait_ge(w_in[1], 16)
            mix_w(1).then_inc(w0_mixed[1], 1)
            pool.wait_ge(w0_rounded[1], 1)
            rest_w(1).then_inc(w0_rest[1], 1)
            pool.wait_ge(w0_rest[1], 1)
            prepare_w(1)
            for m, u in pairs_of_steps(pool, 1, PAIRS // 2):
                prepare_w(2 * m + u)

            def rest_linear(t, u, kt):
                pool.wait_ge(lin_rounded, t + 1)
                pool.tensor_tensor(w_lo[u][:, 0:kt, :], w_raw[u][:, 0:kt, :],
                                   w_hi[u][:, 0:kt, :].bitcast(F32),
                                   ALU.subtract).then_inc(lin_rest, 1)

            def rest_cf(b, chunks=range(2)):
                for c in chunks:
                    pool.wait_ge(cf_rounded, 2 * b + c + 1)
                    pool.tensor_tensor(cf_lo[:, 4 * c:4 * c + 4, :], cf_raw[c][:, :, :],
                                       cf_hi[:, 4 * c:4 * c + 4, :].bitcast(F32),
                                       ALU.subtract).then_inc(cf_rest, 1)

            def rows_power(q, h):
                rows = slice(HB * h, HB * h + HB)
                pool.wait_ge(norm_var, q + 1)
                pool.tensor_tensor(rstd[:, rows, 0], var_eps[:, rows], minus_half[:, :],
                                   ALU.pow).then_inc(norm_rstd, 1)

            def cross_power(b):
                pool.wait_ge(cvar, b + 1)
                pool.tensor_tensor(mv2[:, 3:4], mv2[:, 2:3], minus_half[:, 0:1],
                                   ALU.pow).then_inc(crstd, 1)

            pool.wait_ge(power_set, 1)
            for t in range(4):
                rest_linear(t, t % 2, KT)
            rest_cf(0)
            for m, u in pairs_of_steps(pool, 2, KT // 2):
                rest_linear(2 * m + u, u, KT)
            rows_power(0, 0)
            rest_cf(1)
            rest_cf(2, [0])
            rows_power(1, 1)
            rest_cf(2, [1])
            for m, u in pairs_of_steps(pool, 1, 3):
                cross_power(2 * m + u - 2)
                rest_cf(2 * m + u + 1)
            cross_power(4)
            rest_cf(7)
            cross_power(5)
            pool.wait_ge(lin_rounded, KT + 1)
            pool.tensor_tensor(a_both[:, :, SECOND:P], w_raw[0][:, 0:KT, SECOND:P],
                               a_both[:, :, SECOND:P].bitcast(F32),
                               ALU.subtract).then_inc(lin_rest, 1)
            rest_linear(KT + 1, 1, KT + 1)
            cross_power(6)
            rest_linear(KT + 2, 0, KT + 1)
            cross_power(7)
            for m, u in pairs_of_steps(pool, 6, 8):
                rest_linear(2 * m + u - 1, 1 - u, KT + 1)
            for i in range(2):
                pool.wait_ge(end_rounded, i + 1)
                pool.tensor_tensor(end_lo[:, i, :, :], end_raw[:, i, :, :],
                                   end_hi[:, i, :, :].bitcast(F32),
                                   ALU.subtract).then_inc(end_rest, 1)
            for b in range(B):
                pool.wait_ge(row_var, b + 1)
                pool.tensor_tensor(rstd[:, b, :], var_eps[:, b:b + 1], minus_half[:, 0:1],
                                   ALU.pow).then_inc(row_rstd, 1)


def constants():
    freq = (1.0 / 10000.0 ** (np.arange(0, HD, 2, dtype=np.float32) / np.float32(HD))).astype(np.float32)
    angle = np.arange(S, dtype=np.float32)[None, :] * freq[:, None]
    sin, cos = np.sin(angle), np.cos(angle)
    rotary = np.concatenate([cos + sin, cos - sin] * 2, 0).astype(np.float32)
    causal = np.where(np.tril(np.ones((S, S), bool)), 0.0, MASKED).astype(np.float32)
    route = np.empty((RA, B + 1), np.float32)
    route[:, :B] = np.arange(B)
    route[:, B] = np.arange(RA) // R + 2
    return {"rotary": rotary, "causal": causal, "identity": np.eye(P, dtype=np.float32), "route": route}


def tiles(w):
    return w.reshape(KT, P, KT, P).transpose(2, 1, 0, 3)


def kernel(**inputs):
    import concourse.bacc as bacc
    from concourse.bass_utils import run_bass_kernel_spmd as run

    a = {k: np.asarray(v) for k, v in inputs.items()}
    x, ctx = a["x"], a["ctx_4096"]
    order = np.arange(D).reshape(D // HD, HD // 2, 2).transpose(0, 2, 1).reshape(-1)
    qkv = np.stack([tiles(a["L0_attn_Wq"][:, order]), tiles(a["L0_attn_Wk"][:, order]),
                    tiles(a["L0_attn_Wv"])], 1)
    ffn = np.zeros((KT + 1, P, KT + 1, P), np.float32)
    ffn[0, :, :KT, :RA] = a["L0_ffn_lora_A"].reshape(RA, KT, P).transpose(2, 1, 0)
    ffn[0, :, :KT, SECOND:SECOND + RA] = ffn[0, :, :KT, :RA]
    ffn[1:, :, :KT, :] = tiles(a["L0_ffn_weight"].T)
    ffn[1:, :RA, KT, :] = a["L0_ffn_lora_B"].transpose(0, 2, 1).reshape(RA, KT, P).transpose(1, 0, 2)
    ffn[1:, SECOND:SECOND + RA, KT, :] = ffn[1:, :RA, KT, :]
    ffn[1:, BIAS_ROW, KT, :] = a["L0_ffn_bias"].reshape(KT, P)
    ctx_feat = np.zeros((B, 2, P, KT // 2, LKP), np.float32)
    ctx_feat[..., :LK] = ctx.transpose(0, 2, 1).reshape(B, 2, KT // 2, P, LK).transpose(0, 1, 3, 2, 4)
    starts = a["L0_ffn_lora_start_indices"]
    arrays = {
        "x_feat": x.reshape(B * S, KT, P).transpose(2, 1, 0),
        "x_tok": x.transpose(1, 0, 2).reshape(S, B, KT, P),
        "qkv_w": qkv,
        "wo_w": tiles(a["L0_attn_Wo"]),
        "ffn_w": ffn,
        "ctx_feat": ctx_feat,
        "ctx_tok": ctx.reshape(B, CC, CR, D).transpose(0, 2, 1, 3),
        "starts": np.broadcast_to(starts[None, :], (RA, NA + 1)),
        **constants(),
    }
    arrays = {k: np.ascontiguousarray(v) for k, v in arrays.items()}
    nc = bacc.Bacc("TRN2", target_bir_lowering=False, num_devices=1)
    args = {k: nc.dram_tensor(k, v.shape, mybir.dt.from_np(v.dtype), kind="ExternalInput").ap()
            for k, v in arrays.items()}
    out = nc.dram_tensor("out", (B, S, D), F32, kind="ExternalOutput").ap()
    build(nc, out=out.rearrange("b s (k f) -> b s k f", k=KT), **args)
    r = run(nc, [arrays], core_ids=[0])
    return r.results[0]["out"]
```
